# Optimizing a Trainium2 kernel written in Bass

```python
import numpy as np
import jax
import jax.numpy as jnp

def _softmax(x, axis=-1):
    return jax.nn.softmax(x, axis=axis)
def _gelu(x):
    return jax.nn.gelu(x, approximate=True)
def _silu(x):
    return jax.nn.silu(x)
def _sigmoid(x):
    return jax.nn.sigmoid(x)
def _layernorm(x, axis=-1, eps=1e-5):
    m = jnp.mean(x, axis=axis, keepdims=True)
    v = jnp.var(x, axis=axis, keepdims=True)
    return (x - m) / jnp.sqrt(v + eps)
def _scatter_add(tgt, idx, src, axis=0):
    return tgt.at[idx].add(src)
def _segment_sum(src, seg, n):
    return jax.ops.segment_sum(src, seg, n)

kernel_name = 'mk_conv_seq_d4_conv_nchw16_30ab2a'

def setup_inputs(seed: int = 0):
    np.random.seed(seed)
    _w = jnp.asarray
    def _rec_inputs():
        import jax
        import jax.numpy as jnp
        _gk = jax.random.key(seed)
        x = -0.0003929 + 0.9999 * jax.random.normal(jax.random.fold_in(_gk, 1), (4, 16, 512, 512), jnp.float32)
        return x
    x = _rec_inputs()
    def _L0_conv_setup():
        import jax, jax.numpy as jnp
        import numpy as np
        C = 16
        HEADS = 2
        WS = 8
        HID = 64

        def _aff(x, alpha, beta, color):
            return x @ color.T * alpha + beta
        key = jax.random.key(seed)
        ks = jax.random.split(key, 8)
        B, H, W = (4, 512, 512)
        n = lambda k, s: jax.random.normal(k, s, jnp.float32) * 0.02
        return {'x': jax.random.normal(ks[0], (B, C, H, W), jnp.float32), 'pos_w': n(ks[1], (C, 1, 3, 3)), 'pos_b': jnp.zeros((C,), jnp.float32), 'alpha1': jnp.ones((1, 1, C), jnp.float32), 'beta1': jnp.zeros((1, 1, C), jnp.float32), 'color1': jnp.eye(C, dtype=jnp.float32), 'qkv_w': n(ks[2], (3 * C, C)), 'qkv_b': jnp.zeros((3 * C,), jnp.float32), 'proj_w': n(ks[3], (C, C)), 'proj_b': jnp.zeros((C,), jnp.float32), 'alpha2': jnp.ones((1, 1, C), jnp.float32), 'beta2': jnp.zeros((1, 1, C), jnp.float32), 'color2': jnp.eye(C, dtype=jnp.float32), 'fc1_w': n(ks[4], (HID, C)), 'fc1_b': jnp.zeros((HID,), jnp.float32), 'fc2_w': n(ks[5], (C, HID)), 'fc2_b': jnp.zeros((C,), jnp.float32)}
    _L0_conv_all = _L0_conv_setup()
    _L0_conv_in = {k: v for k, v in _L0_conv_all.items() if k in ('pos_w', 'pos_b', 'alpha1', 'beta1', 'color1', 'qkv_w', 'qkv_b', 'proj_w', 'proj_b', 'alpha2', 'beta2', 'color2', 'fc1_w', 'fc1_b', 'fc2_w', 'fc2_b', )}
    del _L0_conv_all

    def _L1_conv_setup():
        import jax, jax.numpy as jnp
        import numpy as np
        SOBEL_X = jnp.array([[-1.0, 0.0, 1.0], [-2.0, 0.0, 2.0], [-1.0, 0.0, 1.0]], dtype=jnp.float32) / 8.0
        SOBEL_Y = jnp.array([[-1.0, -2.0, -1.0], [0.0, 0.0, 0.0], [1.0, 2.0, 1.0]], dtype=jnp.float32) / 8.0
        TIME_STEPS = 10
        DT = 0.01
        EPS = 1e-06

        def _dwconv(u, k2d):
            C = u.shape[1]
            k = jnp.broadcast_to(k2d[None, None], (C, 1, 3, 3))
            return jax.lax.conv_general_dilated(u, k, window_strides=(1, 1), padding=((1, 1), (1, 1)), dimension_numbers=('NCHW', 'OIHW', 'NCHW'), feature_group_count=C)

        def _derivs(u):
            ux = _dwconv(u, SOBEL_X)
            uy = _dwconv(u, SOBEL_Y)
            uxx = _dwconv(ux, SOBEL_X)
            uxy = _dwconv(ux, SOBEL_Y)
            uyy = _dwconv(uy, SOBEL_Y)
            c = lambda t: jnp.clip(t, -10.0, 10.0)
            return (c(ux), c(uy), c(uxx), c(uxy), c(uyy))
        key = jax.random.key(seed)
        x = jax.random.normal(key, (8, 16, 512, 512), dtype=jnp.float32)
        return {'x': x, 'alpha_param': jnp.float32(0.1), 'beta_param': jnp.float32(0.01)}
    _L1_conv_all = _L1_conv_setup()
    _L1_conv_in = {k: v for k, v in _L1_conv_all.items() if k in ('alpha_param', 'beta_param', )}
    del _L1_conv_all

    def _L2_conv_setup():
        import jax, jax.numpy as jnp
        import numpy as np

        def _conv2d_same(x, w, b):
            y = jax.lax.conv_general_dilated(x, w, window_strides=(1, 1), padding=((1, 1), (1, 1)), dimension_numbers=('NCHW', 'OIHW', 'NCHW'))
            return y + b[None, :, None, None]
        key = jax.random.key(seed)
        ks = jax.random.split(key, 5)
        B, C, H, W = (16, 16, 512, 512)
        K = 3
        bound = float(np.sqrt(1.0 / (C * K * K)))
        x = jax.random.normal(ks[0], (B, C, H, W), dtype=jnp.float32)
        w1 = jax.random.uniform(ks[1], (C, C, K, K), minval=-bound, maxval=bound, dtype=jnp.float32)
        b1 = jax.random.uniform(ks[2], (C,), minval=-bound, maxval=bound, dtype=jnp.float32)
        w2 = jax.random.uniform(ks[3], (C, C, K, K), minval=-bound, maxval=bound, dtype=jnp.float32)
        b2 = jax.random.uniform(ks[4], (C,), minval=-bound, maxval=bound, dtype=jnp.float32)
        return {'x': x, 'w1': w1, 'b1': b1, 'w2': w2, 'b2': b2}
    _L2_conv_all = _L2_conv_setup()
    _L2_conv_in = {k: v for k, v in _L2_conv_all.items() if k in ('w1', 'b1', 'w2', 'b2', )}
    del _L2_conv_all

    def _L3_conv_setup():
        import jax, jax.numpy as jnp
        import numpy as np

        def _conv2d_same(x, w, b):
            y = jax.lax.conv_general_dilated(x, w, window_strides=(1, 1), padding=((1, 1), (1, 1)), dimension_numbers=('NCHW', 'OIHW', 'NCHW'))
            return y + b[None, :, None, None]
        key = jax.random.key(seed)
        ks = jax.random.split(key, 5)
        B, C, H, W = (16, 16, 512, 512)
        K = 3
        bound = float(np.sqrt(1.0 / (C * K * K)))
        x = jax.random.normal(ks[0], (B, C, H, W), dtype=jnp.float32)
        w1 = jax.random.uniform(ks[1], (C, C, K, K), minval=-bound, maxval=bound, dtype=jnp.float32)
        b1 = jax.random.uniform(ks[2], (C,), minval=-bound, maxval=bound, dtype=jnp.float32)
        w2 = jax.random.uniform(ks[3], (C, C, K, K), minval=-bound, maxval=bound, dtype=jnp.float32)
        b2 = jax.random.uniform(ks[4], (C,), minval=-bound, maxval=bound, dtype=jnp.float32)
        return {'x': x, 'w1': w1, 'b1': b1, 'w2': w2, 'b2': b2}
    _L3_conv_all = _L3_conv_setup()
    _L3_conv_in = {k: v for k, v in _L3_conv_all.items() if k in ('w1', 'b1', 'w2', 'b2', )}
    del _L3_conv_all

    return {
        "x": x,
        "L0_conv_pos_w": _L0_conv_in["pos_w"],
        "L0_conv_pos_b": _L0_conv_in["pos_b"],
        "L0_conv_alpha1": _L0_conv_in["alpha1"],
        "L0_conv_beta1": _L0_conv_in["beta1"],
        "L0_conv_color1": _L0_conv_in["color1"],
        "L0_conv_qkv_w": _L0_conv_in["qkv_w"],
        "L0_conv_qkv_b": _L0_conv_in["qkv_b"],
        "L0_conv_proj_w": _L0_conv_in["proj_w"],
        "L0_conv_proj_b": _L0_conv_in["proj_b"],
        "L0_conv_alpha2": _L0_conv_in["alpha2"],
        "L0_conv_beta2": _L0_conv_in["beta2"],
        "L0_conv_color2": _L0_conv_in["color2"],
        "L0_conv_fc1_w": _L0_conv_in["fc1_w"],
        "L0_conv_fc1_b": _L0_conv_in["fc1_b"],
        "L0_conv_fc2_w": _L0_conv_in["fc2_w"],
        "L0_conv_fc2_b": _L0_conv_in["fc2_b"],
        "L1_conv_alpha_param": _L1_conv_in["alpha_param"],
        "L1_conv_beta_param": _L1_conv_in["beta_param"],
        "L2_conv_w1": _L2_conv_in["w1"],
        "L2_conv_b1": _L2_conv_in["b1"],
        "L2_conv_w2": _L2_conv_in["w2"],
        "L2_conv_b2": _L2_conv_in["b2"],
        "L3_conv_w1": _L3_conv_in["w1"],
        "L3_conv_b1": _L3_conv_in["b1"],
        "L3_conv_w2": _L3_conv_in["w2"],
        "L3_conv_b2": _L3_conv_in["b2"],
    }

def reference(x, L0_conv_pos_w, L0_conv_pos_b, L0_conv_alpha1, L0_conv_beta1, L0_conv_color1, L0_conv_qkv_w, L0_conv_qkv_b, L0_conv_proj_w, L0_conv_proj_b, L0_conv_alpha2, L0_conv_beta2, L0_conv_color2, L0_conv_fc1_w, L0_conv_fc1_b, L0_conv_fc2_w, L0_conv_fc2_b, L1_conv_alpha_param, L1_conv_beta_param, L2_conv_w1, L2_conv_b1, L2_conv_w2, L2_conv_b2, L3_conv_w1, L3_conv_b1, L3_conv_w2, L3_conv_b2):
    import jax
    import jax.numpy as jnp
    def _L0_conv_ref(x, pos_w, pos_b, alpha1, beta1, color1, qkv_w, qkv_b, proj_w, proj_b, alpha2, beta2, color2, fc1_w, fc1_b, fc2_w, fc2_b):
        import jax, jax.numpy as jnp
        import numpy as np
        C = 16
        HEADS = 2
        WS = 8
        HID = 64

        def _aff(x, alpha, beta, color):
            return x @ color.T * alpha + beta
        B, Cc, H, W = x.shape
        pos = jax.lax.conv_general_dilated(x, pos_w, window_strides=(1, 1), padding=((1, 1), (1, 1)), dimension_numbers=('NCHW', 'OIHW', 'NCHW'), feature_group_count=Cc)
        x = x + pos + pos_b[None, :, None, None]
        xt = jnp.transpose(x.reshape(B, Cc, H * W), (0, 2, 1))
        shortcut = xt
        y = _aff(xt, alpha1, beta1, color1).reshape(B, H, W, Cc)
        nH, nW = (H // WS, W // WS)
        win = y.reshape(B, nH, WS, nW, WS, Cc).transpose(0, 1, 3, 2, 4, 5)
        win = win.reshape(B * nH * nW, WS * WS, Cc)
        B_, N, _ = win.shape
        hd = Cc // HEADS
        qkv = (win @ qkv_w.T + qkv_b).reshape(B_, N, 3, HEADS, hd)
        qkv = qkv.transpose(2, 0, 3, 1, 4)
        q, k, v = (qkv[0] * hd ** (-0.5), qkv[1], qkv[2])
        attn = jax.nn.softmax(jnp.einsum('bhnd,bhmd->bhnm', q, k), axis=-1)
        out = jnp.einsum('bhnm,bhmd->bhnd', attn, v)
        out = out.transpose(0, 2, 1, 3).reshape(B_, N, Cc)
        out = out @ proj_w.T + proj_b
        out = out.reshape(B, nH, nW, WS, WS, Cc).transpose(0, 1, 3, 2, 4, 5)
        out = out.reshape(B, H * W, Cc)
        x = shortcut + out
        h1 = jax.nn.gelu(_aff(x, alpha2, beta2, color2) @ fc1_w.T + fc1_b, approximate=False)
        x = x + (h1 @ fc2_w.T + fc2_b)
        return jnp.transpose(x, (0, 2, 1)).reshape(B, Cc, H, W)

    def _L1_conv_ref(x, alpha_param, beta_param):
        import jax, jax.numpy as jnp
        import numpy as np
        SOBEL_X = jnp.array([[-1.0, 0.0, 1.0], [-2.0, 0.0, 2.0], [-1.0, 0.0, 1.0]], dtype=jnp.float32) / 8.0
        SOBEL_Y = jnp.array([[-1.0, -2.0, -1.0], [0.0, 0.0, 0.0], [1.0, 2.0, 1.0]], dtype=jnp.float32) / 8.0
        TIME_STEPS = 10
        DT = 0.01
        EPS = 1e-06

        def _dwconv(u, k2d):
            C = u.shape[1]
            k = jnp.broadcast_to(k2d[None, None], (C, 1, 3, 3))
            return jax.lax.conv_general_dilated(u, k, window_strides=(1, 1), padding=((1, 1), (1, 1)), dimension_numbers=('NCHW', 'OIHW', 'NCHW'), feature_group_count=C)

        def _derivs(u):
            ux = _dwconv(u, SOBEL_X)
            uy = _dwconv(u, SOBEL_Y)
            uxx = _dwconv(ux, SOBEL_X)
            uxy = _dwconv(ux, SOBEL_Y)
            uyy = _dwconv(uy, SOBEL_Y)
            c = lambda t: jnp.clip(t, -10.0, 10.0)
            return (c(ux), c(uy), c(uxx), c(uxy), c(uyy))
        alpha = jnp.abs(alpha_param)
        beta = jnp.abs(beta_param)

        def step(u, _):
            ux, uy, uxx, uxy, uyy = _derivs(u)
            g2 = ux * ux + uy * uy
            denK = jnp.maximum(1.0 + g2, EPS)
            K = jnp.clip((uxx * uyy - uxy * uxy) / (denK * denK + EPS), -5.0, 5.0)
            denH = jnp.sqrt(1.0 + g2 + EPS)
            H = ((1.0 + uy * uy) * uxx - 2.0 * ux * uy * uxy + (1.0 + ux * ux) * uyy) / (2.0 * denH ** 3 + EPS)
            H = jnp.clip(H, -5.0, 5.0)
            diff = jnp.clip(alpha * K + beta * H, -1.0, 1.0)
            u = u + DT * diff
            u = jnp.pad(u[:, :, 1:-1, 1:-1], ((0, 0), (0, 0), (1, 1), (1, 1)), mode='edge')
            return (u, None)
        u, _ = jax.lax.scan(step, x, None, length=TIME_STEPS)
        return 0.7 * u + 0.3 * x

    def _L2_conv_ref(x, w1, b1, w2, b2):
        import jax, jax.numpy as jnp
        import numpy as np

        def _conv2d_same(x, w, b):
            y = jax.lax.conv_general_dilated(x, w, window_strides=(1, 1), padding=((1, 1), (1, 1)), dimension_numbers=('NCHW', 'OIHW', 'NCHW'))
            return y + b[None, :, None, None]
        out = _conv2d_same(x, w1, b1)
        out = jax.nn.relu(out)
        out = _conv2d_same(out, w2, b2)
        return out + x

    def _L3_conv_ref(x, w1, b1, w2, b2):
        import jax, jax.numpy as jnp
        import numpy as np

        def _conv2d_same(x, w, b):
            y = jax.lax.conv_general_dilated(x, w, window_strides=(1, 1), padding=((1, 1), (1, 1)), dimension_numbers=('NCHW', 'OIHW', 'NCHW'))
            return y + b[None, :, None, None]
        out = _conv2d_same(x, w1, b1)
        out = jax.nn.relu(out)
        out = _conv2d_same(out, w2, b2)
        return out + x

    def _gn(v, G=8, eps=1e-5):
        B_, C_, H_, W_ = v.shape
        g = v.reshape(B_, G, C_ // G, H_, W_)
        m = jnp.mean(g, axis=(2, 3, 4), keepdims=True)
        s = jnp.var(g, axis=(2, 3, 4), keepdims=True)
        return ((g - m) / jnp.sqrt(s + eps)).reshape(v.shape)

    def _ln_c(v, eps=1e-6):
        m = jnp.mean(v, axis=1, keepdims=True)
        s = jnp.var(v, axis=1, keepdims=True)
        return (v - m) / jnp.sqrt(s + eps)

    def _ln_t(v, eps=1e-5):
        m = jnp.mean(v, axis=-1, keepdims=True)
        s = jnp.var(v, axis=-1, keepdims=True)
        return (v - m) / jnp.sqrt(s + eps)

    def _to_tokens(v):
        B_, C_, H_, W_ = v.shape
        return v.reshape(B_, C_, H_ * W_).transpose(0, 2, 1)
    def _from_tokens(t, like):
        B_, C_, H_, W_ = like.shape
        return t.transpose(0, 2, 1).reshape(B_, C_, H_, W_)

    x = _L0_conv_ref(x, L0_conv_pos_w, L0_conv_pos_b, L0_conv_alpha1, L0_conv_beta1, L0_conv_color1, L0_conv_qkv_w, L0_conv_qkv_b, L0_conv_proj_w, L0_conv_proj_b, L0_conv_alpha2, L0_conv_beta2, L0_conv_color2, L0_conv_fc1_w, L0_conv_fc1_b, L0_conv_fc2_w, L0_conv_fc2_b)
    x = _L1_conv_ref(x, L1_conv_alpha_param, L1_conv_beta_param)
    x = _L2_conv_ref(x, L2_conv_w1, L2_conv_b1, L2_conv_w2, L2_conv_b2)
    x = _L3_conv_ref(x, L3_conv_w1, L3_conv_b1, L3_conv_w2, L3_conv_b2)
    return x


_drawn_inputs = setup_inputs


def setup_inputs(seed=0):
    import zlib

    import numpy as np

    out = dict(_drawn_inputs(seed))
    spreads = {'L0_conv_pos_b': (0.0, 0.1),
     'L0_conv_alpha1': (1.0, 0.6),
     'L0_conv_beta1': (0.0, 0.8),
     'L0_conv_qkv_b': (0.0, 0.8),
     'L0_conv_proj_b': (0.0, 0.1),
     'L0_conv_alpha2': (1.0, 0.6),
     'L0_conv_beta2': (0.0, 2.0),
     'L0_conv_fc1_b': (0.0, 2.0),
     'L0_conv_fc2_b': (0.0, 0.8)}
    factors = {'L0_conv_color1': 8.0,
     'L0_conv_qkv_w': 8.0,
     'L0_conv_proj_w': 7.631,
     'L0_conv_color2': 8.0,
     'L0_conv_fc1_w': 8.0,
     'L0_conv_fc2_w': 5.448,
     'L2_conv_b1': 27.584,
     'L3_conv_b1': 28.224,
     'L2_conv_b2': 24.869,
     'L3_conv_b2': 25.15}
    for name, (base, spread) in spreads.items():
        noise = np.random.default_rng([zlib.crc32(name.encode()), seed]).standard_normal(out[name].shape)
        drawn = base * np.exp(spread * noise) if base else spread * noise
        out[name] = jnp.asarray(drawn.astype(out[name].dtype))
    for name, factor in factors.items():
        out[name] = (out[name] * factor).astype(out[name].dtype)
    return out
```

```python
from contextlib import ExitStack

import concourse.bass as bass
from concourse import mybir

F32 = mybir.dt.float32
F32R = mybir.dt.float32r
ALU = mybir.AluOpType
ACT = mybir.ActivationFunctionType
AX = mybir.AxisListType
STEPS = 10


def attention_stage(nc, x, dst, wt, DST_PAD=2):
    P = 128
    B, C, HP, WP = x.shape
    H, W = HP - 2, WP - 2
    WS = 8
    N = WS * WS
    HEADS, HD = 2, C // 2
    WR = P // C
    WC = 8
    CW = WC * WS
    T = WC * N
    RG = WR // 2
    SROWS = WR * WS
    STRIPS, PAIRS = H // SROWS, W // (2 * CW)
    BODIES = B * STRIPS * PAIRS
    CHUNKS = 2 * BODIES
    HID = 4 * C

    with ExitStack() as ctx:
        def sb(n, shape):
            return ctx.enter_context(nc.sbuf_tensor("att_" + n, shape, F32))

        def sem(n):
            return ctx.enter_context(nc.semaphore("att_" + n))

        def psum(n, shape):
            return ctx.enter_context(nc.psum_tensor("att_" + n, shape, F32))

        color = sb("color", [P, 2, P])
        qkv_raw, qkv_al = sb("qkv_raw", [P, 3, P]), sb("qkv_al", [P, 3, P])
        fc1_raw, fc1_al = sb("fc1_raw", [P, RG, P]), sb("fc1_al", [P, RG, P])
        w_qkv, w_fc1 = sb("w_qkv", [P, 3, P]), sb("w_fc1", [P, RG, P])
        w_proj, w_fc2 = sb("w_proj", [P, P]), sb("w_fc2", [P, RG, P])
        ident = sb("ident", [P, P])
        vec = sb("vec", [P, 26])
        pos_w, pos_b = vec[:, 0:9], vec[:, 9:10]
        alpha1, beta1, alpha2, beta2 = (vec[:, k:k + 1] for k in range(10, 14))
        b_qkv_in, b_proj, b_fc1_in, b_fc2 = vec[:, 14:17], vec[:, 17:18], vec[:, 18:19], vec[:, 19:20]
        q_scale, head_mask = vec[:, 20:22], vec[:, 22:24]
        b_qkv, b_fc1, q_bias = sb("b_qkv", [P, 3]), sb("b_fc1", [P, 1]), sb("q_bias", [P, 2])

        xin = sb("xin", [P, WS + 2, 2 * CW + 2])
        acc = sb("acc", [P, WS, CW])
        xs = sb("xs", [P, 2, T])
        qx = sb("qx", [P, 2, WC, 2, N])
        kx = sb("kx", [P, 2, HEADS, T])
        vx = sb("vx", [P, 2, 2, WC, RG, 2, HEADS, HD])
        pr = sb("pr", [P, RG, WC * HEADS, N])
        mx, sm, rs = sb("mx", [P, RG, WC * HEADS]), sb("sm", [P, RG, WC * HEADS]), sb("rs", [P, RG, WC * HEADS])
        pt = sb("pt", [P, 2, WC, P])
        o_sb = sb("o", [P, T])
        x2 = sb("x2", [P, 2, T])
        hid = sb("hid", [P, RG, T])
        out_rows = sb("out_rows", [P, WS, 2 * CW])

        ps_s = [psum(f"s{k}", [P, WC, P]) for k in range(2)]
        ps_t = psum("t", [P, WC, P])
        ps_o = psum("pv", [P, T])
        ps_m = psum("m", [P, T])

        w_in, setup, w_made, w_ready = sem("w_in"), sem("setup"), sem("w_made"), sem("w_ready")
        x_in, out_stored, conv_step, xs_done = sem("x_in"), sem("out_stored"), sem("conv_step"), sem("xs_done")
        q_made, k_made, v_made = sem("q_made"), sem("k_made"), sem("v_made")
        q_split, k_split, v_split = sem("q_split"), sem("k_split"), sem("v_split")
        s_made, max_done, sub_done, exp_done, sum_done, rec_done, norm_done = (
            sem(n) for n in ("s_made", "max_done", "sub_done", "exp_done", "sum_done", "rec_done", "norm_done"))
        t_made, t_copied, pv_made, o_copied = sem("t_made"), sem("t_copied"), sem("pv_made"), sem("o_copied")
        proj_made, x2_done, f1_made, h_copied, gelu_done, f2_made, y_done, row_copied = (
            sem(n) for n in ("proj_made", "x2_done", "f1_made", "h_copied", "gelu_done", "f2_made", "y_done", "row_copied"))

        def wait(eng, s, value):
            if not isinstance(value, int) or value > 0:
                eng.wait_ge(s, value)

        def every_slot(eng, slot):
            slot(-1, 1, False, False, True)
            slot(0, 0, False, True, True)
            with eng.Fori(1, CHUNKS - 1, 2) as i:
                slot(i, 1, True, True, True)
                slot(i + 1, 0, True, True, True)
            slot(CHUNKS - 1, 1, True, True, False)
            slot(CHUNKS, 0, True, False, False)

        block = ctx.enter_context(nc.Block())

        @block.sync
        def _(sp):
            for t, name in ((color, "color"), (qkv_raw, "qkv"), (fc1_raw, "fc1"), (w_proj, "proj"), (w_fc2, "fc2"),
                            (ident, "ident"), (vec, "vec")):
                sp.dma_start(t.ap() if hasattr(t, "ap") and callable(t.ap) else t[:], wt[name]).then_inc(w_in, 16)

            def place(k):
                return k // (STRIPS * PAIRS), (k // PAIRS) % STRIPS, k % PAIRS

            def load(k):
                b, s, c = place(k)
                wait(sp, conv_step, k * 20)
                for w in range(WR):
                    src = x[bass.ds(b, 1), :, bass.ds(s * SROWS + w * WS, WS + 2), bass.ds(c * (2 * CW), 2 * CW + 2)]
                    sp.dma_start(xin[w * C:(w + 1) * C, :, :], src.rearrange("a c r w -> (a c) r w")).then_inc(x_in, 16)

            def store(k):
                b, s, c = place(k)
                sp.wait_ge(row_copied, (k + 1) * 2)
                for w in range(WR):
                    to = dst[bass.ds(b, 1), :, bass.ds(s * SROWS + w * WS + DST_PAD, WS), bass.ds(c * (2 * CW), 2 * CW)]
                    sp.dma_start(to.rearrange("a c r w -> (a c) r w"), out_rows[w * C:(w + 1) * C, :, :]).then_inc(out_stored, 16)

            load(0)
            load(1)
            with sp.Fori(0, BODIES - 2) as k:
                load(k + 2)
                store(k)
            store(BODIES - 2)
            store(BODIES - 1)
            sp.wait_ge(out_stored, 16 * WR * BODIES)

        @block.tensor
        def _(pe):
            pe.wait_ge(w_in, 16 * 7)
            pe.wait_ge(setup, 2)
            for k in range(3):
                pe.matmul(ps_s[0][:, k, :], color[:, 0, :], qkv_al[:, k, :], start=True, stop=True)
            for k in range(RG):
                pe.matmul(ps_s[1][:, k, :], color[:, 1, :], fc1_al[:, k, :], start=True, stop=True)
            for k in range(3):
                pe.matmul(ps_m[:, k:k + 1], qkv_raw[:, k, :], beta1, start=True, stop=True)
            pe.matmul(ps_m[:, 3:4], fc1_raw[:, 0, :], beta2, start=True, stop=True).then_inc(w_made, 1)
            pe.wait_ge(w_ready, 1)

            def scores(i, par, rg):
                wait(pe, sub_done, i * 4 + (rg - 1))
                for w in range(WC):
                    mm = pe.matmul(ps_s[rg % 2][:, w, :],
                                   qx[32 * rg:32 * rg + 32, par, w].rearrange("p r n -> p (r n)"),
                                   kx[32 * rg:32 * rg + 32, par, :, w * N:(w + 1) * N], start=True, stop=True)
                mm.then_inc(s_made, 1)

            def turn(i, rg):
                pe.wait_ge(norm_done, i * 4 + (rg + 1))
                wait(pe, t_copied, i * 4 + rg)
                for w in range(WC):
                    mm = pe.transpose(ps_t[:, w, :], pr[:, rg, 2 * w:2 * w + 2, :].rearrange("p h m -> p (h m)"), ident[:, :])
                mm.then_inc(t_made, 1)

            def values(i, par, rg):
                pe.wait_ge(t_copied, i * 4 + (rg + 1))
                if rg == 0:
                    wait(pe, o_copied, i)
                for w in range(WC):
                    for r in range(2):
                        mm = pe.matmul(ps_o[32 * rg:32 * rg + 32, w * N:(w + 1) * N],
                                       vx[:, par, r, w, rg].rearrange("p a h d -> p (a h d)"),
                                       pt[:, rg % 2, w, r * N:(r + 1) * N], start=(r == 0), stop=(r == 1))
                mm.then_inc(pv_made, 1)

            def fc1(i, par, j):
                if j == 0:
                    pe.wait_ge(x2_done, i + 1)
                else:
                    pe.wait_ge(h_copied, i * 4 + j)
                pe.matmul(ps_m[:, :], w_fc1[:, j, :], x2[:, par, :], start=True, stop=True).then_inc(f1_made, 1)

            def slot(i, par, prev, cur, nxt):
                o = 1 - par
                if cur:
                    turn(i, 0)
                if prev:
                    fc1(i - 1, o, 0)
                if cur:
                    values(i, par, 0)
                    scores(i, par, 2)
                if prev:
                    fc1(i - 1, o, 1)
                if cur:
                    turn(i, 1)
                    scores(i, par, 3)
                if prev:
                    fc1(i - 1, o, 2)
                if cur:
                    values(i, par, 1)
                if prev:
                    fc1(i - 1, o, 3)
                if cur:
                    turn(i, 2)
                if nxt:
                    pe.wait_ge(xs_done, i + 2)
                    wait(pe, h_copied, i * 4)
                    pe.matmul(ps_m[:, :], w_qkv[:, 0, :], xs[:, o, :], start=True, stop=True).then_inc(q_made, 1)
                if cur:
                    values(i, par, 2)
                if nxt:
                    pe.wait_ge(q_split, i + 2)
                    pe.matmul(ps_m[:, :], w_qkv[:, 1, :], xs[:, o, :], start=True, stop=True).then_inc(k_made, 1)
                if cur:
                    turn(i, 3)
                if nxt:
                    pe.wait_ge(k_split, i + 2)
                    scores(i + 1, o, 0)
                    for w in range(WC):
                        for h in range(HEADS):
                            mm = pe.matmul(ps_m[N * h:N * h + N, w * N:(w + 1) * N], xs[:, o, w * N:(w + 1) * N],
                                           w_qkv[:, 2, :].rearrange("p (r h d) -> p r h d", h=HEADS, d=HD)[:, :, h, :],
                                           start=True, stop=True)
                    mm.then_inc(v_made, 1)
                if cur:
                    values(i, par, 3)
                if nxt:
                    scores(i + 1, o, 1)
                if prev:
                    if nxt:
                        pe.wait_ge(v_split, i + 2)
                    pe.wait_ge(gelu_done, i)
                    for j in range(RG):
                        mm = pe.matmul(ps_m[:, :], w_fc2[:, j, :], hid[:, j, :], start=(j == 0), stop=(j == RG - 1))
                    mm.then_inc(f2_made, 1)
                if cur:
                    pe.wait_ge(o_copied, i + 1)
                    wait(pe, y_done, i)
                    if nxt and not prev:
                        pe.wait_ge(v_split, i + 2)
                    pe.matmul(ps_m[:, :], w_proj[:, :], o_sb[:, :], start=True, stop=True).then_inc(proj_made, 1)

            every_slot(pe, slot)

        @block.scalar
        def _(act):
            act.wait_ge(w_ready, 1)

            def move_t(i, rg):
                act.wait_ge(t_made, i * 4 + (rg + 1))
                wait(act, pv_made, i * 4 + (rg - 1))
                act.activation(pt[:, rg % 2].rearrange("p w n -> p (w n)"), ps_t[:, :, :].rearrange("p w n -> p (w n)"),
                               ACT.Copy).then_inc(t_copied, 1)

            def exps(i, rg):
                act.wait_ge(sub_done, i * 4 + (rg + 1))
                act.activation(pr[:, rg].rearrange("p a m -> p (a m)"), pr[:, rg].rearrange("p a m -> p (a m)"),
                               ACT.Exp).then_inc(exp_done, 1)

            def move_h(i, j):
                act.wait_ge(f1_made, i * 4 + (j + 1))
                if j == 0:
                    wait(act, f2_made, i)
                act.activation(hid[:, j, :], ps_m[:, :], ACT.Copy).then_inc(h_copied, 1)

            def slot(i, par, prev, cur, nxt):
                o = 1 - par
                if cur:
                    move_t(i, 0)
                if prev:
                    move_h(i - 1, 0)
                    move_h(i - 1, 1)
                if cur:
                    exps(i, 2)
                    move_t(i, 1)
                if prev:
                    move_h(i - 1, 2)
                if cur:
                    exps(i, 3)
                if prev:
                    move_h(i - 1, 3)
                if cur:
                    move_t(i, 2)
                if nxt:
                    act.wait_ge(q_made, i + 2)
                    for r in range(2):
                        last = act.activation(qx[:, o, :, r, :], ps_m[:, :].rearrange("p (w n) -> p w n", n=N), ACT.Identity, bias=q_bias[:, r:r + 1], scale=q_scale[:, r:r + 1])
                    last.then_inc(q_split, 1)
                if cur:
                    move_t(i, 3)
                if prev:
                    act.wait_ge(h_copied, i * 4)
                    act.activation(hid[:, :, :].rearrange("p j t -> p (j t)"), hid[:, :, :].rearrange("p j t -> p (j t)"),
                                   ACT.Gelu, bias=b_fc1[:, 0:1]).then_inc(gelu_done, 1)
                if nxt:
                    exps(i + 1, 0)
                if cur:
                    act.wait_ge(pv_made, i * 4 + 4)
                    act.activation(o_sb[:, :], ps_o[:, :], ACT.Identity, bias=b_qkv[:, 2:3]).then_inc(o_copied, 1)
                if nxt:
                    exps(i + 1, 1)
                if prev:
                    act.wait_ge(y_done, i)
                    if par == 1:
                        wait(act, out_stored, (i - 1) * (16 * WR // 2))
                    act.activation(out_rows[:, :, o * CW:(o + 1) * CW].rearrange("p y (w x) -> p w y x", x=WS),
                                   x2[:, o, :].rearrange("p (w y x) -> p w y x", y=WS, x=WS), ACT.Copy).then_inc(row_copied, 1)

            every_slot(act, slot)

        @block.gpsimd
        def _(pool):
            def norm(i, rg):
                pool.wait_ge(rec_done, i * 4 + (rg + 1))
                pool.tensor_tensor(pr[:, rg], pr[:, rg], rs[:, rg, :].unsqueeze(2).to_broadcast([P, WC * HEADS, N]),
                                   ALU.mult).then_inc(norm_done, 1)

            def slot(i, par, prev, cur, nxt):
                if cur:
                    norm(i, 1)
                    norm(i, 2)
                    norm(i, 3)
                if nxt:
                    norm(i + 1, 0)

            every_slot(pool, slot)

        @block.vector
        def _(dve):
            dve.memset(vx[:].rearrange("p a b c d e f g -> p (a b c d e f g)"), 0.0).then_inc(setup, 1)
            dve.wait_ge(w_in, 16 * 7)
            dve.tensor_scalar(qkv_al[:, :, :], qkv_raw[:, :, :], alpha1, None, ALU.mult)
            dve.tensor_scalar(fc1_al[:, :, :], fc1_raw[:, :, :], alpha2, None, ALU.mult).then_inc(setup, 1)
            dve.wait_ge(w_made, 1)
            dve.tensor_copy(w_qkv[:, :, :], ps_s[0][:, 0:3, :])
            dve.tensor_copy(w_fc1[:, :, :], ps_s[1][:, 0:RG, :])
            dve.tensor_tensor(b_fc1[:, :], ps_m[:, 3:4], b_fc1_in, ALU.add)
            dve.tensor_tensor(b_qkv[:, :], ps_m[:, 0:3], b_qkv_in, ALU.add).then_inc(setup, 1)
            dve.wait_ge(setup, 3)
            dve.tensor_scalar(q_bias[:, :], q_scale, b_qkv[:, 0:1], None, ALU.mult).then_inc(w_ready, 1)

            TAPS = [(dy, dx) for dy in range(3) for dx in range(3) if (dy, dx) != (1, 1)]

            def conv(i, par, steps):
                def view(dy, dx):
                    return xin[:, dy:dy + WS, par * CW + dx:par * CW + dx + CW]
                for st in steps:
                    if st == 0:
                        dve.wait_ge(x_in, (i + (2 - par)) * (8 * WR))
                        dve.tensor_scalar(acc[:, :, :], view(1, 1), pos_w[:, 4:5], pos_b, ALU.mult, ALU.add).then_inc(conv_step, 1)
                    elif st < 9:
                        dy, dx = TAPS[st - 1]
                        dve.wait_ge(conv_step, i * 10 + st)
                        dve.scalar_tensor_tensor(out=acc[:, :, :], in0=view(dy, dx), scalar=pos_w[:, 3 * dy + dx:3 * dy + dx + 1],
                                                 in1=acc[:, :, :], op0=ALU.mult, op1=ALU.add).then_inc(conv_step, 1)
                    else:
                        dve.wait_ge(conv_step, i * 10 + st)
                        turned = [a.rearrange("p y (w x) -> p w y x", x=WS) for a in (acc[:, :, :], view(1, 1))]
                        dve.tensor_tensor(xs[:, par, :].rearrange("p (w y x) -> p w y x", y=WS, x=WS), *turned,
                                          ALU.add).then_inc(conv_step, 1)
                        dve.wait_ge(conv_step, i * 10 + 10)
                        dve.sem_inc(xs_done, 1)

            def top(i, rg):
                dve.wait_ge(s_made, i * 4 + (rg + 1))
                sc = ps_s[rg % 2][:, :, :].rearrange("p w (h m) -> p (w h) m", h=HEADS)
                dve.tensor_reduce(mx[:, rg, :], sc, AX.X, ALU.max).then_inc(max_done, 1)
                wait(dve, t_made, i * 4 + (rg - 3))
                dve.wait_ge(max_done, i * 4 + (rg + 1))
                dve.tensor_tensor(pr[:, rg], sc, mx[:, rg, :].unsqueeze(2).to_broadcast([P, WC * HEADS, N]),
                                  ALU.subtract).then_inc(sub_done, 1)

            def total(i, rg):
                dve.wait_ge(exp_done, i * 4 + (rg + 1))
                dve.tensor_reduce(sm[:, rg, :], pr[:, rg], AX.X, ALU.add).then_inc(sum_done, 1)
                dve.wait_ge(sum_done, i * 4 + (rg + 1))
                dve.reciprocal(rs[:, rg, :], sm[:, rg, :]).then_inc(rec_done, 1)

            def slot(i, par, prev, cur, nxt):
                o = 1 - par
                if prev:
                    dve.wait_ge(proj_made, i)
                    wait(dve, row_copied, i - 1)
                    dve.scalar_tensor_tensor(out=x2[:, o, :], in0=ps_m[:, :], scalar=b_proj, in1=xs[:, o, :],
                                             op0=ALU.add, op1=ALU.add).then_inc(x2_done, 1)
                if cur:
                    total(i, 1)
                if nxt:
                    conv(i + 1, o, range(0, 4))
                if cur:
                    top(i, 2)
                if nxt:
                    conv(i + 1, o, range(4, 7))
                if cur:
                    top(i, 3)
                if nxt:
                    conv(i + 1, o, range(7, 10))
                if cur:
                    total(i, 2)
                    total(i, 3)
                if nxt:
                    dve.wait_ge(k_made, i + 2)
                    for h in range(HEADS):
                        last = dve.tensor_scalar(kx[:, o, h, :], ps_m[:, :], b_qkv[:, 1:2], head_mask[:, h:h + 1], ALU.add, ALU.mult)
                    last.then_inc(k_split, 1)
                    top(i + 1, 0)
                    dve.wait_ge(v_made, i + 2)
                    for h in range(HEADS):
                        hp = slice(N * h, N * h + N)
                        vp = ps_m[hp, :].rearrange("p (w g r d) -> p w g r d", w=WC, g=RG, r=2)
                        for r in range(2):
                            last = dve.tensor_copy(vx[hp, o, r, :, :, r, h, :], vp[:, :, :, r, :])
                    last.then_inc(v_split, 1)
                    total(i + 1, 0)
                    top(i + 1, 1)
                if prev:
                    dve.wait_ge(f2_made, i)
                    dve.scalar_tensor_tensor(out=x2[:, o, :], in0=ps_m[:, :], scalar=b_fc2, in1=x2[:, o, :],
                                             op0=ALU.add, op1=ALU.add).then_inc(y_done, 1)

            every_slot(dve, slot)


def attention_weights(a):
    import numpy as np
    C, WR, HID = 16, 8, 64
    f = np.float32

    def blocks(m):
        i, o = m.shape
        z = np.zeros((WR, i, WR, o), m.dtype)
        for r in range(WR):
            z[r, :, r, :] = m
        return z.reshape(WR * i, WR * o)

    def tile(v):
        return np.tile(np.asarray(v).reshape(-1), 128 // np.asarray(v).size).reshape(128, 1)

    qkv = a["qkv_w"]
    p = np.arange(128)
    row = (p // C) % 2
    head = (p // (C // 2)) % 2
    scale = (C // 2) ** -0.5
    vec = np.concatenate(
        [np.tile(a["pos_w"].reshape(C, 9), (WR, 1)), tile(a["pos_b"]), tile(a["alpha1"]), tile(a["beta1"]), tile(a["alpha2"]),
         tile(a["beta2"])] + [tile(a["qkv_b"][C * k:C * k + C]) for k in range(3)] +
        [tile(a["proj_b"]), tile(a["fc1_b"]), tile(a["fc2_b"])] +
        [np.where(row == r, scale, 0).astype(f).reshape(128, 1) for r in range(2)] +
        [np.where(head == h, 1, 0).astype(f).reshape(128, 1) for h in range(2)] + [np.zeros((128, 2), f)], axis=1).astype(f)
    fc2 = blocks(np.ascontiguousarray(a["fc2_w"].T)).reshape(WR * HID // 128, 128, 128).transpose(1, 0, 2)
    return dict(
        color=np.stack([blocks(a["color1"]), blocks(a["color2"])], axis=1),
        qkv=np.stack([blocks(np.ascontiguousarray(qkv[C * k:C * k + C].T)) for k in range(3)], axis=1),
        fc1=blocks(np.ascontiguousarray(a["fc1_w"].T)).reshape(128, 4, 128),
        proj=blocks(np.ascontiguousarray(a["proj_w"].T)),
        fc2=np.ascontiguousarray(fc2),
        ident=np.eye(128, dtype=f),
        vec=vec)


def surface_consts():
    import numpy as np
    P = 128
    profiles = {
        "ux": ([1, 2, 1], 8, (-1, 1)),
        "uy": ([-1, 0, 1], 8, (1, 2)),
        "uxx": ([1, 4, 6, 4, 1], 64, (1, -2)),
        "uxy": ([-1, -2, 0, 2, 1], 64, (-1, -2, 2, 1)),
        "uyy": ([1, 0, -2, 0, 1], 64, (1, 4, 6)),
    }
    mats = []
    for taps, div, weights in profiles.values():
        r = len(taps) // 2
        band = np.zeros((P, P), np.float32)
        for m in range(P):
            for o, v in enumerate(taps):
                k = m + o - r
                if 0 <= k < P:
                    band[k, m] = v / div
        mats += [w * band for w in weights]
    return np.stack(mats, axis=1).astype(np.float32)


def surface_mask(slots, edge_slot, halo, blocks, block_rows):
    import numpy as np
    m = np.zeros((128, slots), np.float32)
    m[halo:128 - halo, :] = 0.01
    m[:, edge_slot] = 0.0
    for b in range(blocks):
        m[b * block_rows + halo:(b + 1) * block_rows - halo, edge_slot] = 0.01
    return m


def surface_stage(nc, x1, u10, mats, mask, alpha_in, beta_in, STEPS):
    P = 128
    IMAGES, HP, W = x1.shape
    HALO = 2
    OWN = P - 2 * HALO
    KT = (HP - 2 * HALO) // OWN
    REST = HP - 2 * HALO - KT * OWN
    BLOCK = REST + 2 * HALO
    GI = 8
    HI = GI // 2
    GROUPS = IMAGES // GI
    UNITS = HI * KT + 1
    FIRST = HI // 2
    REST_UNIT = FIRST * KT
    TOTAL = GROUPS * STEPS * UNITS
    NM = mats.shape[1]
    EPS = 1e-6
    TAPS = {
        "p": [(-1, 0), (1, 1)],
        "q": [(-1, 2), (0, 3), (1, 2)],
        "A": [(-2, 4), (0, 5), (2, 4)],
        "B": [(-2, 6), (-1, 7), (1, 8), (2, 9)],
        "C": [(-2, 10), (-1, 11), (0, 12), (1, 11), (2, 10)],
    }

    def unit0(j):
        return j * KT + (1 if j >= FIRST else 0)

    with ExitStack() as ctx:
        def sb(name, shape, dt=F32):
            return ctx.enter_context(nc.sbuf_tensor(name, shape, dt))

        def sem(name):
            return ctx.enter_context(nc.semaphore(name))

        u = sb("surf_u", [P, UNITS, 2, W])
        parts = sb("surf_parts", [P, 2, 2, 2, W + 4], F32R)
        matf = sb("surf_matf", [P, NM, P])
        matr = sb("surf_matr", [P, NM, P], F32R)
        dt_mask = sb("surf_dt", [P, UNITS])
        ab = sb("surf_ab", [P, 2])
        absab = sb("surf_absab", [P, 2])
        cst = sb("surf_cst", [P, 3])
        clips = sb("surf_clips", [P, 4])
        bufs = {n: sb("surf_" + n, [P, 2, 2, W]) for n in
                ("pc", "qc", "Ac", "Bc", "Cc", "p2", "q2", "B2", "g", "rK", "rH", "nK", "m")}
        banks = [ctx.enter_context(nc.psum_tensor(f"surf_ps{i}", [P, 2, W], F32)) for i in range(4)]
        alpha, beta = absab[:, 0:1], absab[:, 1:2]
        one, onee, eps = cst[:, 0:1], cst[:, 1:2], cst[:, 2:3]

        init_loaded, init_set, cst_set, init_done, mats_round = sem("init_loaded"), sem("init_set"), sem("cst_set"), sem("init_done"), sem("mats_round")
        batches, moved, unit_ready, updated = sem("batches"), sem("moved"), sem("unit_ready"), sem("updated")
        hi_done, lo_done = sem("hi_done"), sem("lo_done")
        made = {n: sem("made_" + n) for n in "pqABC"}
        copied = {n: sem("copied_" + n) for n in "qABC"}
        clipped = {n: sem("clipped_" + n) for n in "pqABC"}
        squared = {n: sem("squared_" + n) for n in "pqB"}
        g_sum, ac_done, numk, pq_done, t12_done, numh = (sem(n) for n in ("g_sum", "ac_done", "numk", "pq_done", "t12_done", "numh"))
        sS, sL3, sL, sE, sL2, rk_done, rh_done = (sem(n) for n in ("den_sq", "den_ln", "g_ln", "g_pow", "h_ln", "rk_done", "rh_done"))
        t1_done, t2_done, m_done = sem("t1_done"), sem("t2_done"), sem("m_done")
        k_scaled, k_clipped, h_scaled, h_clipped, s_done, s_clipped, u_moved = (sem(n) for n in ("k_scaled", "k_clipped", "h_scaled", "h_clipped", "s_done", "s_clipped", "u_stepped"))

        def flat(ap):
            return ap.rearrange("p t w -> p (t w)")

        def buf(n, par):
            return flat(bufs[n][:, par])

        def bank(name, par):
            return banks[(5 * par + list(TAPS).index(name)) % 4]

        def last_in_bank(j, par):
            names = list(TAPS)
            if j == 4:
                return names[0], 0
            o = 1 - par
            return names[max(x for x in range(5) if (5 * o + x) % 4 == (5 * par + j) % 4)], 1

        block = ctx.enter_context(nc.Block())

        @block.sync
        def _(sp):
            sp.dma_start(matf[:, :, :], mats).then_inc(init_loaded, 16)
            sp.dma_start(dt_mask[:, :], mask).then_inc(init_loaded, 16)
            sp.dma_start(ab[:, 0:1], alpha_in.to_broadcast([P, 1])).then_inc(init_loaded, 16)
            sp.dma_start(ab[:, 1:2], beta_in.to_broadcast([P, 1])).then_inc(init_loaded, 16)
            sp.wait_ge(init_done, 1)

            def landed(c):
                sp.wait_ge(moved, c)
                sp.sem_inc(batches, 1)

            def load_pair(g, j):
                for t in range(2):
                    img = g * GI + (j + t * HI)
                    for k in range(KT):
                        sp.dma_start(u[:, unit0(j) + k, t, :],
                                     x1[bass.ds(img, 1), OWN * k:OWN * k + P, :].rearrange("a p w -> p (a w)")).then_inc(moved, 16)

            def load_rests(g):
                for t in range(2):
                    for j in range(HI):
                        img = g * GI + (j + t * HI)
                        sp.dma_start(u[j * BLOCK:(j + 1) * BLOCK, REST_UNIT, t, :],
                                     x1[bass.ds(img, 1), OWN * KT:OWN * KT + BLOCK, :].rearrange("a p w -> p (a w)")).then_inc(moved, 16)

            def store_pair(g, j):
                for t in range(2):
                    img = g * GI + (j + t * HI)
                    for k in range(KT):
                        sp.dma_start(u10[bass.ds(img, 1), HALO + OWN * k:HALO + OWN * (k + 1), :].rearrange("a p w -> p (a w)"),
                                     u[HALO:P - HALO, unit0(j) + k, t, :]).then_inc(moved, 16)

            def store_rests(g):
                for t in range(2):
                    for j in range(HI):
                        img = g * GI + (j + t * HI)
                        sp.dma_start(u10[bass.ds(img, 1), HALO + OWN * KT:HALO + OWN * KT + REST, :].rearrange("a p w -> p (a w)"),
                                     u[j * BLOCK + HALO:(j + 1) * BLOCK - HALO, REST_UNIT, t, :]).then_inc(moved, 16)

            def exchange_pair(j):
                a, b = unit0(j), unit0(j) + KT - 1
                n = 0
                if KT > 1:
                    sp.dma_start(u[0:HALO, a + 1:b + 1], u[P - 2 * HALO:P - HALO, a:b]).then_inc(moved, 16)
                    sp.dma_start(u[P - HALO:P, a:b], u[HALO:2 * HALO, a + 1:b + 1]).then_inc(moved, 16)
                    n += 2
                sp.dma_start(u[HALO:HALO + 1, a], u[HALO + 1:HALO + 2, a]).then_inc(moved, 16)
                return n + 1

            def exchange_rest(j):
                b, r = unit0(j) + KT - 1, j * BLOCK
                sp.dma_start(u[r:r + HALO, REST_UNIT], u[P - 2 * HALO:P - HALO, b]).then_inc(moved, 16)
                sp.dma_start(u[P - HALO:P, b], u[r + HALO:r + 2 * HALO, REST_UNIT]).then_inc(moved, 16)
                return 2

            def last_rows():
                for j in range(HI):
                    r = j * BLOCK + HALO + REST - 1
                    sp.dma_start(u[r:r + 1, REST_UNIT], u[r - 1:r, REST_UNIT]).then_inc(moved, 16)
                return HI

            loads_pair, rests = 2 * KT, 2 * HI
            for j in range(FIRST):
                load_pair(0, j)
            load_rests(0)
            for j in range(FIRST, HI):
                load_pair(0, j)
            n0 = 16 * (loads_pair * HI + rests)
            sp.wait_ge(moved, n0)
            sp.sem_inc(unit_ready, UNITS)

            per_pair = 3 if KT > 1 else 1
            EX = 16 * (per_pair * HI + 2 * HI + HI)
            STEP_A = REST_UNIT + 1

            def exchange(done, before):
                c = before
                for j in range(FIRST):
                    sp.wait_ge(updated, done + unit0(j) + KT)
                    c = c + 16 * exchange_pair(j)
                    landed(c)
                sp.wait_ge(updated, done + REST_UNIT + 1)
                c = c + 16 * last_rows()
                for j in range(FIRST):
                    c = c + 16 * exchange_rest(j)
                landed(c)
                sp.sem_inc(unit_ready, STEP_A - 1)
                for j in range(FIRST, HI):
                    sp.wait_ge(updated, done + unit0(j) + KT)
                    c = c + 16 * exchange_pair(j)
                    c = c + 16 * exchange_rest(j)
                    landed(c)
                sp.sem_inc(unit_ready, UNITS - STEP_A + 1)

            def boundary(g, done, before, load):
                c = before
                for j in range(FIRST):
                    sp.wait_ge(updated, done + unit0(j) + KT)
                    sp.dma_start(u[HALO:HALO + 1, unit0(j)], u[HALO + 1:HALO + 2, unit0(j)]).then_inc(moved, 16)
                    c = c + 16
                    landed(c)
                    store_pair(g, j)
                    c = c + 16 * loads_pair
                    landed(c)
                    if load:
                        load_pair(g + 1, j)
                        c = c + 16 * loads_pair
                        landed(c)
                sp.wait_ge(updated, done + REST_UNIT + 1)
                c = c + 16 * last_rows()
                landed(c)
                store_rests(g)
                c = c + 16 * rests
                landed(c)
                if load:
                    load_rests(g + 1)
                    c = c + 16 * rests
                    landed(c)
                    sp.sem_inc(unit_ready, STEP_A)
                for j in range(FIRST, HI):
                    sp.wait_ge(updated, done + unit0(j) + KT)
                    sp.dma_start(u[HALO:HALO + 1, unit0(j)], u[HALO + 1:HALO + 2, unit0(j)]).then_inc(moved, 16)
                    c = c + 16
                    landed(c)
                    store_pair(g, j)
                    c = c + 16 * loads_pair
                    landed(c)
                    if load:
                        load_pair(g + 1, j)
                        c = c + 16 * loads_pair
                        landed(c)
                if load:
                    sp.sem_inc(unit_ready, UNITS - STEP_A)

            BD = 16 * (2 * (loads_pair * HI + rests) + 2 * HI)
            GROUP_MOVES = (STEPS - 1) * EX + BD
            if GROUPS > 1:
                with sp.Fori(0, GROUPS - 1) as g:
                    with sp.Fori(0, STEPS - 1) as s:
                        exchange(g * (STEPS * UNITS) + s * UNITS, g * GROUP_MOVES + s * EX + n0)
                    boundary(g, g * (STEPS * UNITS) + (STEPS - 1) * UNITS, g * GROUP_MOVES + ((STEPS - 1) * EX + n0), True)
            last = GROUPS - 1
            with sp.Fori(0, STEPS - 1) as s:
                exchange(s * UNITS + last * STEPS * UNITS, s * EX + (last * GROUP_MOVES + n0))
            boundary(last, last * STEPS * UNITS + (STEPS - 1) * UNITS, last * GROUP_MOVES + (STEPS - 1) * EX + n0, False)

        @block.tensor
        def _(pe):
            pe.wait_ge(mats_round, 1)

            def unit(n, par, first):
                pe.wait_ge(lo_done, n + 1)
                for j, (name, taps) in enumerate(TAPS.items()):
                    ps = bank(name, par)
                    if not first or j == 4:
                        before, back = last_in_bank(j, par)
                        pe.wait_ge((clipped if before == "p" else copied)[before], n - back + 1)
                    count = 2 * len(taps)
                    for t in range(2):
                        i = 0
                        for off, mat in taps:
                            for part in range(2):
                                mm = pe.matmul(ps[:, t, :], matr[:, mat, :], parts[:, par, part, t, off + 2:off + 2 + W],
                                               start=(i == 0), stop=(i == count - 1))
                                i += 1
                    mm.then_inc(made[name], 1)

            unit(0, 0, True)
            unit(1, 1, False)
            with pe.Fori(2, TOTAL, 2) as n:
                unit(n, 0, False)
                unit(n + 1, 1, False)

        @block.scalar
        def _(act):
            act.preload_act_table_set("natural_log_exp_and_others")

            def slot(n, par, new=True, mid=True, nxt=True, wait_ready=True):
                o = 1 - par
                if mid:
                    act.wait_ge(made["C"], n)
                    if not isinstance(n, int) or n > 2:
                        act.wait_ge(s_done, n - 2)
                    act.activation(buf("Cc", o), flat(bank("C", o)[:, :, :]), ACT.Copy).then_inc(copied["C"], 1)
                    act.wait_ge(clipped["B"], n)
                    act.activation(buf("B2", o), buf("Bc", o), ACT.Square).then_inc(squared["B"], 1)
                if nxt:
                    act.activation(parts[:, o, 0, :, 2:W + 2], u[:, bass.ds((n + 1) % UNITS, 1), :, :].rearrange("p a t w -> p (a t) w"),
                                   ACT.Copy).then_inc(hi_done, 1)
                if mid:
                    act.wait_ge(g_sum, n)
                    act.activation(buf("rK", o), buf("g", o), ACT.Square, bias=1.0).then_inc(sS, 1)
                    act.activation(buf("rH", o), buf("g", o), ACT.Ln, bias=1.0 + EPS).then_inc(sL, 1)
                if new:
                    act.wait_ge(made["q"], n + 1)
                    act.activation(buf("qc", par), flat(bank("q", par)[:, :, :]), ACT.Copy).then_inc(copied["q"], 1)
                if mid:
                    act.wait_ge(sS, n)
                    act.activation(buf("rK", o), buf("rK", o), ACT.Ln, bias=EPS).then_inc(sL3, 1)
                    act.wait_ge(sL, n)
                    act.activation(buf("rH", o), buf("rH", o), ACT.Exp, scale=1.5).then_inc(sE, 1)
                if new:
                    act.wait_ge(clipped["p"], n + 1)
                    act.activation(buf("p2", par), buf("pc", par), ACT.Square).then_inc(squared["p"], 1)
                    act.wait_ge(made["A"], n + 1)
                    act.activation(buf("Ac", par), flat(bank("A", par)[:, :, :]), ACT.Copy).then_inc(copied["A"], 1)
                if mid:
                    act.wait_ge(sL3, n)
                    act.activation(buf("rK", o), buf("rK", o), ACT.Exp, scale=-1.0).then_inc(rk_done, 1)
                    act.wait_ge(sE, n)
                    act.activation(buf("rH", o), buf("rH", o), ACT.Ln, bias=EPS, scale=2.0).then_inc(sL2, 1)
                if new:
                    act.wait_ge(clipped["q"], n + 1)
                    act.activation(buf("q2", par), buf("qc", par), ACT.Square).then_inc(squared["q"], 1)
                    if wait_ready:
                        act.wait_ge(unit_ready, n + 3)
                    act.wait_ge(made["B"], n + 1)
                    act.activation(buf("Bc", par), flat(bank("B", par)[:, :, :]), ACT.Copy).then_inc(copied["B"], 1)
                if mid:
                    act.wait_ge(sL2, n)
                    act.activation(buf("rH", o), buf("rH", o), ACT.Exp, scale=-1.0).then_inc(rh_done, 1)

            act.wait_ge(unit_ready, 2)
            act.activation(parts[:, 0, 0, :, 2:W + 2], u[:, 0, :, :], ACT.Copy).then_inc(hi_done, 1)
            slot(0, 0, mid=False)
            slot(1, 1)
            with act.Fori(2, TOTAL - 2, 2) as n:
                slot(n, 0)
                slot(n + 1, 1)
            slot(TOTAL - 2, 0, wait_ready=False)
            slot(TOTAL - 1, 1, nxt=False, wait_ready=False)
            slot(TOTAL, 0, new=False, nxt=False)

        @block.gpsimd
        def _(pool):
            def slot(n, par, first=False):
                o = 1 - par
                g, p2, q2 = buf("g", o), buf("p2", o), buf("q2", o)
                nk, ac, cc, bc, m = buf("nK", o), buf("Ac", o), buf("Cc", o), buf("Bc", o), buf("m", o)
                pool.wait_ge(squared["q"], n)
                pool.tensor_tensor(g, p2, q2, ALU.add).then_inc(g_sum, 1)
                pool.wait_ge(clipped["q"], n)
                pool.tensor_tensor(m, buf("pc", o), buf("qc", o), ALU.mult).then_inc(pq_done, 1)
                pool.wait_ge(clipped["C"], n)
                pool.tensor_tensor(nk, ac, cc, ALU.mult).then_inc(ac_done, 1)
                pool.wait_ge(t1_done, n)
                pool.wait_ge(t2_done, n)
                pool.tensor_tensor(p2, q2, p2, ALU.add).then_inc(t12_done, 1)
                pool.wait_ge(ac_done, n)
                pool.wait_ge(squared["B"], n)
                pool.tensor_tensor(nk, nk, buf("B2", o), ALU.subtract).then_inc(numk, 1)
                pool.wait_ge(m_done, n)
                pool.wait_ge(t12_done, n)
                pool.tensor_tensor(cc, p2, m, ALU.add).then_inc(numh, 1)

            slot(1, 1)
            slot(2, 0)
            with pool.Fori(2, TOTAL, 2) as n:
                slot(n + 1, 1)
                slot(n + 2, 0)

        @block.vector
        def _(dve):
            dve.memset(parts[:, :, :, :, :].rearrange("p a b t w -> p (a b t w)").bitcast(F32), 0.0).then_inc(init_set, 1)
            dve.memset(u[:, REST_UNIT].rearrange("p t w -> p (t w)"), 0.0).then_inc(init_set, 1)
            dve.memset(cst[:, 0:1], 1.0).then_inc(init_set, 1)
            dve.memset(cst[:, 1:2], 1.0 + EPS).then_inc(init_set, 1)
            dve.memset(cst[:, 2:3], EPS).then_inc(init_set, 1)
            dve.wait_ge(init_set, 5)
            dve.tensor_scalar(cst[:, 0:1], cst[:, 0:1], 1.0, None, ALU.mult).then_inc(cst_set, 1)
            dve.sem_inc(init_done, 1)
            dve.wait_ge(init_loaded, 64)
            dve.tensor_copy(matr[:, :, :], matf[:, :, :]).then_inc(mats_round, 1)
            dve.scalar_tensor_tensor(out=absab[:, :], in0=ab[:, :], scalar=-1.0, in1=ab[:, :], op0=ALU.mult, op1=ALU.max).then_inc(init_set, 1)
            dve.wait_ge(init_set, 6)

            CLIP = (10.0, -10.0, ALU.min, ALU.max)

            def low(n, o):
                dve.wait_ge(hi_done, n + 1)
                dve.tensor_tensor(parts[:, o, 1, :, 2:W + 2], u[:, bass.ds(n % UNITS, 1), :, :].rearrange("p a t w -> p (a t) w"),
                                  parts[:, o, 0, :, 2:W + 2].bitcast(F32), ALU.subtract).then_inc(lo_done, 1)

            def slot(n, par, new=True, mid=True, end=True, nxt=True):
                o = 1 - par
                if mid:
                    dve.wait_ge(copied["C"], n)
                    dve.tensor_scalar(buf("Cc", o), buf("Cc", o), *CLIP).then_inc(clipped["C"], 1)
                if end:
                    dve.wait_ge(rk_done, n - 1)
                    dve.wait_ge(numk, n - 1)
                    dve.scalar_tensor_tensor(out=buf("nK", par), in0=buf("nK", par), scalar=alpha, in1=buf("rK", par),
                                             op0=ALU.mult, op1=ALU.mult).then_inc(k_scaled, 1)
                if new:
                    dve.wait_ge(made["p"], n + 1)
                    dve.tensor_scalar(buf("pc", par), flat(bank("p", par)[:, :, :]), *CLIP).then_inc(clipped["p"], 1)
                if nxt:
                    low(n + 1, o)
                if mid:
                    dve.wait_ge(g_sum, n)
                    dve.wait_ge(clipped["C"], n)
                    dve.scalar_tensor_tensor(out=buf("p2", o), in0=buf("p2", o), scalar=1.0, in1=buf("Cc", o),
                                             op0=ALU.add, op1=ALU.mult).then_inc(t2_done, 1)
                if end:
                    dve.wait_ge(rh_done, n - 1)
                    dve.wait_ge(numh, n - 1)
                    dve.scalar_tensor_tensor(out=buf("Cc", par), in0=buf("Cc", par), scalar=beta, in1=buf("rH", par),
                                             op0=ALU.mult, op1=ALU.mult).then_inc(h_scaled, 1)
                    dve.wait_ge(k_scaled, n - 1)
                    dve.tensor_scalar(buf("nK", par), buf("nK", par), clip_a[:, 0:1], clip_a[:, 1:2], ALU.min, ALU.max).then_inc(k_clipped, 1)
                if mid:
                    dve.scalar_tensor_tensor(out=buf("q2", o), in0=buf("q2", o), scalar=1.0, in1=buf("Ac", o),
                                             op0=ALU.add, op1=ALU.mult).then_inc(t1_done, 1)
                if end:
                    dve.wait_ge(h_scaled, n - 1)
                    dve.tensor_scalar(buf("Cc", par), buf("Cc", par), clip_b[:, 0:1], clip_b[:, 1:2], ALU.min, ALU.max).then_inc(h_clipped, 1)
                if new:
                    dve.wait_ge(copied["q"], n + 1)
                    dve.tensor_scalar(buf("qc", par), buf("qc", par), *CLIP).then_inc(clipped["q"], 1)
                if mid:
                    dve.wait_ge(pq_done, n)
                    dve.scalar_tensor_tensor(out=buf("m", o), in0=buf("m", o), scalar=-2.0, in1=buf("Bc", o),
                                             op0=ALU.mult, op1=ALU.mult).then_inc(m_done, 1)
                if end:
                    dve.wait_ge(h_clipped, n - 1)
                    dve.wait_ge(k_clipped, n - 1)
                    dve.tensor_tensor(buf("nK", par), buf("nK", par), buf("Cc", par), ALU.add).then_inc(s_done, 1)
                if new:
                    dve.wait_ge(copied["A"], n + 1)
                    dve.tensor_scalar(buf("Ac", par), buf("Ac", par), *CLIP).then_inc(clipped["A"], 1)
                if end:
                    dve.wait_ge(s_done, n - 1)
                    dve.tensor_scalar(buf("nK", par), buf("nK", par), 1.0, -1.0, ALU.min, ALU.max).then_inc(s_clipped, 1)
                    dve.wait_ge(s_clipped, n - 1)
                    un = u[:, bass.ds((n - 2) % UNITS, 1), :, :].rearrange("p a t w -> p (a t w)")
                    dve.scalar_tensor_tensor(out=un, in0=buf("nK", par), scalar=dt_mask[:, bass.ds((n - 2) % UNITS, 1)], in1=un,
                                             op0=ALU.mult, op1=ALU.add).then_inc(u_moved, 1)
                    uv = u[:, bass.ds((n - 2) % UNITS, 1), :, :].rearrange("p a t w -> p (a t) w")
                    dve.wait_ge(u_moved, n - 1)
                    dve.tensor_scalar(uv[:, :, 0:W:W - 1], uv[:, :, 1:W - 1:W - 3], 1.0, None, ALU.mult).then_inc(updated, 1)
                if new:
                    dve.wait_ge(copied["B"], n + 1)
                    dve.tensor_scalar(buf("Bc", par), buf("Bc", par), *CLIP).then_inc(clipped["B"], 1)

            clip_a, clip_b = clips[:, 0:2], clips[:, 2:4]
            for i, v in enumerate((5.0, -5.0)):
                dve.tensor_scalar(clips[:, i:i + 3:2], absab[:, :], v, None, ALU.mult).then_inc(init_set, 1)
            dve.wait_ge(init_set, 8)
            low(0, 0)
            slot(0, 0, mid=False, end=False)
            slot(1, 1, end=False)
            with dve.Fori(2, TOTAL - 2, 2) as n:
                slot(n, 0)
                slot(n + 1, 1)
            slot(TOTAL - 2, 0)
            slot(TOTAL - 1, 1, nxt=False)
            slot(TOTAL, 0, new=False, nxt=False)
            slot(TOTAL + 1, 1, new=False, mid=False, nxt=False)


RIN, ROUT = 8, 6


def conv_stage(nc, name, src, dst, weights, bias, relu, residual=None, mix_with=None, mixed=None, dst_pad=0):
    P = 128
    B, C, HP, W = src.shape
    PAD = 2
    H = HP - 2 * PAD
    M = C * ROUT
    NB = 4
    TILES = -(-H // ROUT)
    LOOPS = (TILES - 1) // NB
    with ExitStack() as ctx:
        def sb(n, shape):
            return ctx.enter_context(nc.sbuf_tensor(f"{name}_{n}", shape, F32))

        def sem(n):
            return ctx.enter_context(nc.semaphore(f"{name}_{n}"))

        w_sb = sb("w", [P, 3, M])
        b_sb = sb("b", [M, 1])
        rows = sb("rows", [P, NB, B, W + 2])
        outs = sb("outs", [M, NB, B, W])
        res = sb("res", [M, NB, B, W]) if residual is not None else None
        us = sb("us", [P, NB, B, W]) if mix_with is not None else None
        xs = sb("xs", [P, NB, B, W]) if mix_with is not None else None
        ps = [ctx.enter_context(nc.psum_tensor(f"{name}_ps{i}", [M, B, W], F32)) for i in range(2)]
        w_loaded, padded = sem("w_loaded"), sem("padded")
        loaded = [sem(f"loaded{b}") for b in range(NB)]
        stored = [sem(f"stored{b}") for b in range(NB)]
        scaled, mix_done, conv_done, out_done = sem("scaled"), sem("mix_done"), sem("conv_done"), sem("out_done")
        if mixed is not None:
            y_stored = [sem(f"y_stored{b}") for b in range(NB)]

        def wait(eng, s, value):
            if not isinstance(value, int) or value > 0:
                eng.wait_ge(s, value)

        def every_tile(eng, body):
            for b in range(NB):
                body(0, b, ROUT * b)
            if LOOPS > 1:
                with eng.Fori(1, LOOPS) as i:
                    for b in range(NB):
                        body(i, b, i * (NB * ROUT) + ROUT * b)
            for t in range(NB * LOOPS, TILES):
                body(t // NB, t % NB, min(ROUT * t, H - ROUT))

        def dram_rows(a, b, row, n):
            return a[b, :, bass.ds(row, n), :]

        block = ctx.enter_context(nc.Block())

        @block.sync
        def _(sp):
            sp.dma_start(w_sb[:, :, :], weights).then_inc(w_loaded, 16)
            sp.dma_start(b_sb[:, :], bias).then_inc(w_loaded, 16)
            sp.wait_ge(padded, 1)

            def body(i, b, row):
                t = i * NB + b
                if mix_with is None:
                    wait(sp, conv_done, t - NB + 1)
                    for bb in range(B):
                        sp.dma_start(rows[:, b, bb, 1:W + 1], dram_rows(src, bb, row + PAD - 1, RIN)).then_inc(loaded[b], 16)
                else:
                    wait(sp, mix_done, t - NB + 1)
                    for bb in range(B):
                        sp.dma_start(us[:, b, bb, :], dram_rows(src, bb, row + PAD - 1, RIN)).then_inc(loaded[b], 16)
                        sp.dma_start(xs[:, b, bb, :], dram_rows(mix_with, bb, row + PAD - 1, RIN)).then_inc(loaded[b], 16)
                if residual is not None:
                    wait(sp, out_done, t - NB + 1)
                    for bb in range(B):
                        sp.dma_start(res[:, b, bb, :], dram_rows(residual, bb, row + PAD, ROUT)).then_inc(loaded[b], 16)

            every_tile(sp, body)

        NLOAD = 16 * B * (1 + (mix_with is not None) + (residual is not None))

        @block.tensor
        def _(pe):
            pe.wait_ge(w_loaded, 32)

            def body(i, b, row):
                t = i * NB + b
                if mix_with is None:
                    pe.wait_ge(loaded[b], (i + 1) * NLOAD)
                else:
                    pe.wait_ge(mix_done, t + 1)
                wait(pe, out_done, t - 1)
                for bb in range(B):
                    for dx in range(3):
                        mm = pe.matmul(ps[b % 2][:, bb, :], w_sb[:, dx, :], rows[:, b, bb, dx:dx + W],
                                       start=(dx == 0), stop=(dx == 2))
                mm.then_inc(conv_done, 1)

            every_tile(pe, body)

        @block.vector
        def _(dve):
            dve.memset(rows[:, :, :, :].rearrange("p n b w -> p (n b w)"), 0.0).then_inc(padded, 1)
            if mix_with is not None:
                dve.wait_ge(padded, 1)
            if residual is not None:
                dve.wait_ge(w_loaded, 32)

            def mix_body(i, b, row):
                t = i * NB + b
                dve.wait_ge(loaded[b], (i + 1) * NLOAD)
                dve.tensor_scalar(xs[:, b], xs[:, b], 0.3, None, ALU.mult).then_inc(scaled, 1)
                wait(dve, y_stored[b], i * (16 * B))
                wait(dve, conv_done, t - NB + 1)
                dve.wait_ge(scaled, t + 1)
                dve.scalar_tensor_tensor(out=rows[:, b, :, 1:W + 1], in0=us[:, b], scalar=0.7, in1=xs[:, b],
                                         op0=ALU.mult, op1=ALU.add).then_inc(mix_done, 1)

            def sum_body(i, b, row):
                t = i * NB + b
                dve.wait_ge(conv_done, t + 1)
                dve.wait_ge(loaded[b], (i + 1) * NLOAD)
                wait(dve, stored[b], i * (16 * B))
                dve.scalar_tensor_tensor(out=outs[:, b], in0=ps[b % 2][:, :, :], scalar=b_sb[:, 0:1], in1=res[:, b],
                                         op0=ALU.add, op1=ALU.add).then_inc(out_done, 1)

            if mix_with is not None:
                every_tile(dve, mix_body)
            if residual is not None:
                every_tile(dve, sum_body)

        @block.scalar
        def _(act):
            act.wait_ge(w_loaded, 32)

            def body(i, b, row):
                t = i * NB + b
                if relu:
                    act.wait_ge(conv_done, t + 1)
                    wait(act, stored[b], i * (16 * B))
                    act.activation(outs[:, b].rearrange("p b w -> p (b w)"), ps[b % 2][:, :, :].rearrange("p b w -> p (b w)"),
                                   ACT.Relu, bias=b_sb[:, 0:1]).then_inc(out_done, 1)
                act.wait_ge(out_done, t + 1)
                if isinstance(i, int) and t == TILES - 1:
                    act.wait_ge(stored[(t - 1) % NB], ((t - 1) // NB + 1) * (16 * B))
                for bb in range(B):
                    act.dma_start(dram_rows(dst, bb, row + dst_pad, ROUT), outs[:, b, bb, :]).then_inc(stored[b], 16)

            every_tile(act, body)
            for b in range(NB):
                act.wait_ge(stored[b], ((TILES - 1 - b) // NB + 1) * (16 * B))

        if mixed is not None:
            @block.gpsimd
            def _(pool):
                def body(i, b, row):
                    t = i * NB + b
                    pool.wait_ge(mix_done, t + 1)
                    if not isinstance(i, int) or t > 0:
                        pool.wait_ge(y_stored[(b - 1) % NB], (i + 1 if b else i) * (16 * B))
                    for bb in range(B):
                        pool.dma_start(dram_rows(mixed, bb, row + PAD - 1, RIN), rows[:, b, bb, 1:W + 1]).then_inc(y_stored[b], 16)

                every_tile(pool, body)
                for b in range(NB):
                    pool.wait_ge(y_stored[b], ((TILES - 1 - b) // NB + 1) * (16 * B))


def conv_weights(w):
    import numpy as np
    co, ci = w.shape[:2]
    m = np.zeros((ci, RIN, 3, co, ROUT), w.dtype)
    for r in range(ROUT):
        for dy in range(3):
            m[:, r + dy, :, :, r] = w[:, :, dy, :].transpose(1, 2, 0)
    return m.reshape(ci * RIN, 3, co * ROUT)


def conv_bias(b):
    import numpy as np
    return np.repeat(b, ROUT).reshape(-1, 1)


def clear_halos(nc, zeros, arrays):
    with nc.semaphore("halos_cleared") as cleared, nc.semaphore("zeroed") as zeroed, \
            nc.sbuf_tensor("zero_rows", [64, zeros], F32) as rows, nc.Block() as block:
        @block.vector
        def _(dve):
            dve.memset(rows[:, :], 0.0).then_inc(zeroed, 1)

        @block.sync
        def _(sp):
            sp.wait_ge(zeroed, 1)
            for a in arrays:
                h = a.shape[2]
                images = a.rearrange("b c h w -> (b c) h w")
                for r in (0, h - 2):
                    sp.dma_start(images[:, r:r + 2, :].rearrange("i r w -> i (r w)"), rows[:, :]).then_inc(cleared, 16)
            sp.wait_ge(cleared, 16 * 2 * len(arrays))


def build(nc, ins, out):
    B, C, H, W = out.shape

    def scratch(name):
        return nc.dram_tensor(name, (B, C, H + 4, W), F32, kind="Internal").ap()

    attended, flowed, mixed, hidden, middle = (scratch(n) for n in ("attended", "flowed", "mixed", "hidden", "middle"))
    clear_halos(nc, 2 * W, (attended, flowed, hidden, middle))
    attention_stage(nc, ins["x"], attended, {n[4:]: ins[n] for n in ins if n.startswith("att_")})

    def images(a):
        return a.rearrange("b c h w -> (b c) h w")

    surface_stage(nc, images(attended), images(flowed), ins["surf_mats"], ins["surf_mask"], ins["alpha"], ins["beta"], STEPS)
    conv_stage(nc, "conv1", flowed, hidden, ins["w_conv1"], ins["b_conv1"], True, mix_with=attended, mixed=mixed, dst_pad=2)
    conv_stage(nc, "conv2", hidden, middle, ins["w_conv2"], ins["b_conv2"], False, residual=mixed, dst_pad=2)
    conv_stage(nc, "conv3", middle, hidden, ins["w_conv3"], ins["b_conv3"], True, dst_pad=2)
    conv_stage(nc, "conv4", hidden, out, ins["w_conv4"], ins["b_conv4"], False, residual=middle)


def kernel(**inputs):
    import numpy as _np
    import concourse.bacc as _bacc
    from concourse.bass_utils import run_bass_kernel_spmd as _run

    given = {n: _np.asarray(a) for n, a in inputs.items()}
    H = given["x"].shape[2]
    own, halo = 124, 2
    tiles = H // own
    rest = H - own * tiles
    arrays = {
        "x": _np.pad(given["x"], ((0, 0), (0, 0), (1, 1), (1, 1))),
        "surf_mats": surface_consts(),
        "surf_mask": surface_mask(4 * tiles + 1, 2 * tiles, halo, 4, rest + 2 * halo),
        "alpha": given["L1_conv_alpha_param"].reshape(1, 1),
        "beta": given["L1_conv_beta_param"].reshape(1, 1),
    }
    l0 = {n[len("L0_conv_"):]: a for n, a in given.items() if n.startswith("L0_conv_")}
    arrays.update({"att_" + n: a for n, a in attention_weights(l0).items()})
    for k, n in enumerate(("L2_conv_%s1", "L2_conv_%s2", "L3_conv_%s1", "L3_conv_%s2")):
        arrays[f"w_conv{k + 1}"] = conv_weights(given[n % "w"])
        arrays[f"b_conv{k + 1}"] = conv_bias(given[n % "b"])
    arrays = {n: _np.ascontiguousarray(a) for n, a in arrays.items()}

    nc = _bacc.Bacc("TRN2", target_bir_lowering=False, num_devices=1)
    ins = {n: nc.dram_tensor("in_" + n, a.shape, F32, kind="ExternalInput").ap() for n, a in arrays.items()}
    out = nc.dram_tensor("out_0", given["x"].shape, F32, kind="ExternalOutput").ap()
    build(nc, ins, out)
    r = _run(nc, [{"in_" + n: a for n, a in arrays.items()}], core_ids=[0])
    return r.results[0]["out_0"]
```

```python
from contextlib import ExitStack

import concourse.bass as bass
from concourse import mybir

F32 = mybir.dt.float32
F32R = mybir.dt.float32r
ALU = mybir.AluOpType
ACT = mybir.ActivationFunctionType
AX = mybir.AxisListType
STEPS = 10


def attention_stage(nc, x, dst, wt, DST_PAD=2):
    P = 128
    B, C, HP, WP = x.shape
    H, W = HP - 2, WP - 2
    WS = 8
    N = WS * WS
    HEADS, HD = 2, C // 2
    WR = P // C
    WC = 8
    CW = WC * WS
    T = WC * N
    RG = WR // 2
    SROWS = WR * WS
    STRIPS, PAIRS = H // SROWS, W // (2 * CW)
    BODIES = B * STRIPS * PAIRS
    CHUNKS = 2 * BODIES

    with ExitStack() as ctx:
        def sb(n, shape):
            return ctx.enter_context(nc.sbuf_tensor("att_" + n, shape, F32))

        def sem(n):
            return ctx.enter_context(nc.semaphore("att_" + n))

        def psum(n, shape):
            return ctx.enter_context(nc.psum_tensor("att_" + n, shape, F32))

        color = sb("color", [P, 2, P])
        qkv_raw, qkv_al = sb("qkv_raw", [P, 3, P]), sb("qkv_al", [P, 3, P])
        fc1_raw, fc1_al = sb("fc1_raw", [P, RG, P]), sb("fc1_al", [P, RG, P])
        w_qkv, w_fc1 = sb("w_qkv", [P, 3, P]), sb("w_fc1", [P, RG, P])
        w_proj, w_fc2 = sb("w_proj", [P, P]), sb("w_fc2", [P, RG, P])
        ident = sb("ident", [P, P])
        vec = sb("vec", [P, 24])
        pos_w, pos_b = vec[:, 0:9], vec[:, 9:10]
        alpha1, beta1, alpha2, beta2 = (vec[:, k:k + 1] for k in range(10, 14))
        b_qkv_in, b_proj, b_fc1_in, b_fc2 = vec[:, 14:17], vec[:, 17:18], vec[:, 18:19], vec[:, 19:20]
        q_scale, head_mask = vec[:, 20:22], vec[:, 22:24]
        b_qkv, b_fc1 = sb("b_qkv", [P, 3]), sb("b_fc1", [P, 1])
        q_bias, k_bias = sb("q_bias", [P, 2]), sb("k_bias", [P, 2])

        xin = sb("xin", [P, 2, WS + 2, CW + 2])
        acc = sb("acc", [P, WS, CW])
        xs = sb("xs", [P, 2, T])
        qx = sb("qx", [P, 2, WC, 2, N])
        kx = sb("kx", [P, 2, HEADS, T])
        vx = sb("vx", [P, 2, 2, WC, RG, 2, HEADS, HD])
        pr = sb("pr", [P, RG, WC * HEADS, N])
        mx, sm, rs = sb("mx", [P, RG, WC * HEADS]), sb("sm", [P, RG, WC * HEADS]), sb("rs", [P, RG, WC * HEADS])
        pt = sb("pt", [P, 2, WC, P])
        o_sb = sb("o", [P, T])
        x2 = sb("x2", [P, 2, T])
        hid = sb("hid", [P, 2, RG, T])
        y_sb = sb("y", [P, T])
        out_rows = sb("out_rows", [P, WS, 2 * CW])

        ps_s = [psum(f"s{k}", [P, WC, P]) for k in range(2)]
        ps_t = psum("t", [P, WC // 2, P])
        ps_o = psum("pv", [P, T])
        ps_m = [psum(f"m{k}", [P, T]) for k in range(2)]

        w_in, setup, w_made, w_ready = sem("w_in"), sem("setup"), sem("w_made"), sem("w_ready")
        x_in, out_stored, conv_step = [sem("x_even"), sem("x_odd")], sem("out_stored"), sem("conv_step")
        q_made, k_made, v_made = sem("q_made"), sem("k_made"), sem("v_made")
        q_split, k_split, v_split = sem("q_split"), sem("k_split"), sem("v_split")
        s_made, max_done, sub_done, exp_done, sum_done, rec_done, norm_done = (
            sem(n) for n in ("s_made", "max_done", "sub_done", "exp_done", "sum_done", "rec_done", "norm_done"))
        t_made, t_copied, pv_made, o_copied = sem("t_made"), sem("t_copied"), sem("pv_made"), sem("o_copied")
        proj_made, x2_done, f1_made, h_copied, gelu_done, f2_made, y_done, row_copied = (
            sem(n) for n in ("proj_made", "x2_done", "f1_made", "h_copied", "gelu_done", "f2_made", "y_done", "row_copied"))

        STEPS_OF_CONV = 10
        TAPS = [(1, 1)] + [(dy, dx) for dy in range(3) for dx in range(3) if (dy, dx) != (1, 1)]

        def wait(eng, s, value):
            if not isinstance(value, int) or value > 0:
                eng.wait_ge(s, value)

        def every_slot(eng, slot):
            for i in range(-2, 5):
                slot(i, i % 2)
            with eng.Fori(5, CHUNKS - 3, 2) as i:
                slot(i, 1)
                slot(i + 1, 0)
            for i in range(CHUNKS - 3, CHUNKS + 3):
                slot(i, i % 2)

        def there(c):
            return not isinstance(c, int) or 0 <= c < CHUNKS

        block = ctx.enter_context(nc.Block())

        @block.sync
        def _(sp):
            for t, name in ((color, "color"), (qkv_raw, "qkv"), (fc1_raw, "fc1"), (w_proj, "proj"), (w_fc2, "fc2"),
                            (ident, "ident"), (vec, "vec")):
                sp.dma_start(t[:], wt[name]).then_inc(w_in, 16)

            def place(k, n):
                return k // (STRIPS * n), (k // n) % STRIPS, k % n

            def load(i, par):
                b, s, c = place(i, 2 * PAIRS)
                wait(sp, conv_step, (i - 1) * STEPS_OF_CONV)
                for w in range(WR):
                    src = x[bass.ds(b, 1), :, bass.ds(s * SROWS + w * WS, WS + 2), bass.ds(c * CW, CW + 2)]
                    sp.dma_start(xin[w * C:(w + 1) * C, par, :, :], src.rearrange("a c r w -> (a c) r w")).then_inc(x_in[par], 16)

            def store(k):
                b, s, c = place(k, PAIRS)
                sp.wait_ge(row_copied, (k + 1) * 2)
                for w in range(WR):
                    to = dst[bass.ds(b, 1), :, bass.ds(s * SROWS + w * WS + DST_PAD, WS), bass.ds(c * (2 * CW), 2 * CW)]
                    sp.dma_start(to.rearrange("a c r w -> (a c) r w"), out_rows[w * C:(w + 1) * C, :, :]).then_inc(out_stored, 16)

            for i in range(7):
                load(i, i % 2)
            with sp.Fori(0, BODIES - 4) as k:
                load(k * 2 + 7, 1)
                store(k)
                load(k * 2 + 8, 0)
            load(CHUNKS - 1, 1)
            for k in range(BODIES - 4, BODIES):
                store(k)
            sp.wait_ge(out_stored, 16 * WR * BODIES)

        @block.tensor
        def _(pe):
            pe.wait_ge(w_in, 16 * 7)
            pe.wait_ge(setup, 2)
            for k in range(3):
                pe.matmul(ps_s[0][:, k, :], color[:, 0, :], qkv_al[:, k, :], start=True, stop=True)
            for k in range(RG):
                pe.matmul(ps_s[1][:, k, :], color[:, 1, :], fc1_al[:, k, :], start=True, stop=True)
            for k in range(3):
                pe.matmul(ps_m[0][:, k:k + 1], qkv_raw[:, k, :], beta1, start=True, stop=True)
            pe.matmul(ps_m[0][:, 3:4], fc1_raw[:, 0, :], beta2, start=True, stop=True).then_inc(w_made, 1)
            pe.wait_ge(w_ready, 1)

            def scores(i, par, rg):
                if not there(i):
                    return
                if rg == 0:
                    pe.wait_ge(q_split, i + 1)
                    pe.wait_ge(k_split, i + 1)
                wait(pe, sub_done, i * 4 + (rg - 1))
                for w in range(WC):
                    mm = pe.matmul(ps_s[rg % 2][:, w, :],
                                   qx[32 * rg:32 * rg + 32, par, w].rearrange("p r n -> p (r n)"),
                                   kx[32 * rg:32 * rg + 32, par, :, w * N:(w + 1) * N], start=True, stop=True)
                mm.then_inc(s_made, 1)

            def turn(i, rg, half):
                if not there(i):
                    return
                if half == 0:
                    pe.wait_ge(norm_done, i * 4 + (rg + 1))
                wait(pe, t_copied, i * 8 + (rg * 2 + half))
                for w in range(WC // 2):
                    a = 2 * (w + half * (WC // 2))
                    mm = pe.transpose(ps_t[:, w, :], pr[:, rg, a:a + 2, :].rearrange("p h m -> p (h m)"), ident[:, :])
                mm.then_inc(t_made, 1)

            def values(i, par, rg):
                if not there(i):
                    return
                pe.wait_ge(t_copied, i * 8 + (rg * 2 + 2))
                if rg == 0:
                    pe.wait_ge(v_split, i + 1)
                    wait(pe, o_copied, i)
                for w in range(WC):
                    for r in range(2):
                        mm = pe.matmul(ps_o[32 * rg:32 * rg + 32, w * N:(w + 1) * N],
                                       vx[:, par, r, w, rg].rearrange("p a h d -> p (a h d)"),
                                       pt[:, rg % 2, w, r * N:(r + 1) * N], start=(r == 0), stop=(r == 1))
                mm.then_inc(pv_made, 1)

            def fc1(i, par, j):
                if not there(i):
                    return
                bank = 1 - j % 2
                if j == 0:
                    pe.wait_ge(x2_done, i + 1)
                elif j == 1:
                    wait(pe, y_done, i - 1)
                elif j == 2:
                    if there(i + 2):
                        pe.wait_ge(q_split, i + 3)
                    else:
                        pe.wait_ge(h_copied, i * 4 + 1)
                elif there(i + 2):
                    pe.wait_ge(k_split, i + 3)
                else:
                    pe.wait_ge(h_copied, i * 4 + 2)
                pe.matmul(ps_m[bank][:, :], w_fc1[:, j, :], x2[:, par, :], start=True, stop=True).then_inc(f1_made, 1)

            def query(i, par):
                if not there(i):
                    return
                pe.wait_ge(conv_step, (i + 1) * STEPS_OF_CONV)
                if there(i - 2):
                    pe.wait_ge(h_copied, (i - 2) * 4 + 1)
                else:
                    wait(pe, v_split, i)
                pe.matmul(ps_m[1][:, :], w_qkv[:, 0, :], xs[:, par, :], start=True, stop=True).then_inc(q_made, 1)

            def key(i, par):
                if not there(i):
                    return
                if there(i - 2):
                    pe.wait_ge(h_copied, (i - 2) * 4 + 2)
                else:
                    wait(pe, k_split, i)
                pe.matmul(ps_m[0][:, :], w_qkv[:, 1, :], xs[:, par, :], start=True, stop=True).then_inc(k_made, 1)

            def value(i, par):
                if not there(i):
                    return
                if there(i - 2):
                    pe.wait_ge(h_copied, (i - 2) * 4 + 3)
                else:
                    pe.wait_ge(q_split, i + 1)
                for w in range(WC):
                    for h in range(HEADS):
                        mm = pe.matmul(ps_m[1][N * h:N * h + N, w * N:(w + 1) * N], xs[:, par, w * N:(w + 1) * N],
                                       w_qkv[:, 2, :].rearrange("p (r h d) -> p r h d", h=HEADS, d=HD)[:, :, h, :],
                                       start=True, stop=True)
                mm.then_inc(v_made, 1)

            def fc2(i, par, pairs):
                if not there(i):
                    return
                if pairs[0] == 0:
                    pe.wait_ge(gelu_done, i + 1)
                    if there(i + 1):
                        pe.wait_ge(h_copied, (i + 2) * 4)
                    else:
                        pe.wait_ge(y_done, i)
                for j in pairs:
                    mm = pe.matmul(ps_m[0][:, :], w_fc2[:, j, :], hid[:, par, j, :], start=(j == 0), stop=(j == RG - 1))
                if pairs[-1] == RG - 1:
                    mm.then_inc(f2_made, 1)

            def project(i):
                if not there(i):
                    return
                pe.wait_ge(o_copied, i + 1)
                if there(i + 1):
                    pe.wait_ge(v_split, i + 2)
                else:
                    pe.wait_ge(h_copied, (i - 1) * 4 + 3)
                pe.matmul(ps_m[1][:, :], w_proj[:, :], o_sb[:, :], start=True, stop=True).then_inc(proj_made, 1)

            def slot(i, par):
                o = 1 - par
                turn(i, 0, 0)
                scores(i, par, 2)
                turn(i, 0, 1)
                fc1(i - 1, o, 0)
                values(i, par, 0)
                fc1(i - 1, o, 1)

                turn(i, 1, 0)
                query(i + 1, o)
                scores(i, par, 3)
                turn(i, 1, 1)
                key(i + 1, o)
                values(i, par, 1)
                fc1(i - 1, o, 2)

                turn(i, 2, 0)
                scores(i + 1, o, 0)
                turn(i, 2, 1)
                fc1(i - 1, o, 3)
                values(i, par, 2)
                value(i + 1, o)

                turn(i, 3, 0)
                scores(i + 1, o, 1)
                turn(i, 3, 1)
                fc2(i - 2, par, (0,))
                values(i, par, 3)
                fc2(i - 2, par, (1, 2, 3))
                project(i)

            every_slot(pe, slot)

        @block.scalar
        def _(act):
            act.wait_ge(w_ready, 1)

            def move_t(i, rg, half):
                if not there(i):
                    return
                act.wait_ge(t_made, i * 8 + (rg * 2 + half + 1))
                if half == 0:
                    wait(act, pv_made, i * 4 + (rg - 1))
                ws = slice(half * (WC // 2), (half + 1) * (WC // 2))
                act.activation(pt[:, rg % 2, ws].rearrange("p w n -> p (w n)"), ps_t[:, :, :].rearrange("p w n -> p (w n)"),
                               ACT.Copy).then_inc(t_copied, 1)

            def exps(i, rg):
                if not there(i):
                    return
                act.wait_ge(sub_done, i * 4 + (rg + 1))
                act.activation(pr[:, rg].rearrange("p a m -> p (a m)"), pr[:, rg].rearrange("p a m -> p (a m)"),
                               ACT.Exp).then_inc(exp_done, 1)

            def move_h(i, par, j):
                if not there(i):
                    return
                act.wait_ge(f1_made, i * 4 + (j + 1))
                if j == 0:
                    wait(act, f2_made, i - 1)
                act.activation(hid[:, par, j, :], ps_m[1 - j % 2][:, :], ACT.Copy).then_inc(h_copied, 1)

            def split_q(i, par):
                if not there(i):
                    return
                act.wait_ge(q_made, i + 1)
                for r in range(2):
                    last = act.activation(qx[:, par, :, r, :], ps_m[1][:, :].rearrange("p (w n) -> p w n", n=N),
                                          ACT.Identity, bias=q_bias[:, r:r + 1], scale=q_scale[:, r:r + 1])
                last.then_inc(q_split, 1)

            def split_k(i, par):
                if not there(i):
                    return
                act.wait_ge(k_made, i + 1)
                for h in range(HEADS):
                    last = act.activation(kx[:, par, h, :], ps_m[0][:, :], ACT.Identity, bias=k_bias[:, h:h + 1],
                                          scale=head_mask[:, h:h + 1])
                last.then_inc(k_split, 1)

            def split_v(i, par):
                if not there(i):
                    return
                act.wait_ge(v_made, i + 1)
                for h in range(HEADS):
                    hp = slice(N * h, N * h + N)
                    vp = ps_m[1][hp, :].rearrange("p (w g r d) -> p w g r d", w=WC, g=RG, r=2)
                    for r in range(2):
                        last = act.activation(vx[hp, par, r, :, :, r, h, :], vp[:, :, :, r, :], ACT.Copy)
                last.then_inc(v_split, 1)

            def move_o(i):
                if not there(i):
                    return
                act.wait_ge(pv_made, i * 4 + 4)
                act.activation(o_sb[:, :], ps_o[:, :], ACT.Identity, bias=b_qkv[:, 2:3]).then_inc(o_copied, 1)

            def gelu(i, par):
                if not there(i):
                    return
                act.wait_ge(h_copied, (i + 1) * 4)
                act.activation(hid[:, par].rearrange("p j t -> p (j t)"), hid[:, par].rearrange("p j t -> p (j t)"),
                               ACT.Gelu, bias=b_fc1[:, 0:1]).then_inc(gelu_done, 1)

            def to_rows(i, par):
                if not there(i):
                    return
                if par == 0:
                    wait(act, out_stored, i * (8 * WR))
                act.wait_ge(y_done, i + 1)
                act.activation(out_rows[:, :, par * CW:(par + 1) * CW].rearrange("p y (w x) -> p w y x", x=WS),
                               y_sb[:, :].rearrange("p (w y x) -> p w y x", y=WS, x=WS), ACT.Copy).then_inc(row_copied, 1)

            def slot(i, par):
                o = 1 - par
                move_t(i, 0, 0)
                exps(i, 1)
                move_t(i, 0, 1)
                move_h(i - 1, o, 0)
                move_h(i - 1, o, 1)
                to_rows(i - 3, o)
                exps(i, 2)

                move_t(i, 1, 0)
                split_q(i + 1, o)
                move_t(i, 1, 1)
                split_k(i + 1, o)
                move_h(i - 1, o, 2)
                exps(i, 3)

                move_t(i, 2, 0)
                move_t(i, 2, 1)
                move_h(i - 1, o, 3)
                split_v(i + 1, o)

                move_t(i, 3, 0)
                exps(i + 1, 0)
                move_t(i, 3, 1)
                move_o(i)
                gelu(i - 1, o)
                act.preload_act_table_set("exp_and_others")

            every_slot(act, slot)

        @block.gpsimd
        def _(pool):
            def norm(i, rg):
                if not there(i):
                    return
                pool.wait_ge(rec_done, i * 4 + (rg + 1))
                pool.tensor_tensor(pr[:, rg], pr[:, rg], rs[:, rg, :].unsqueeze(2).to_broadcast([P, WC * HEADS, N]),
                                   ALU.mult).then_inc(norm_done, 1)

            def slot(i, par):
                norm(i, 1)
                norm(i, 2)
                norm(i, 3)
                norm(i + 1, 0)

            every_slot(pool, slot)

        @block.vector
        def _(dve):
            dve.memset(vx[:].rearrange("p a b c d e f g -> p (a b c d e f g)"), 0.0).then_inc(setup, 1)
            dve.wait_ge(w_in, 16 * 7)
            dve.tensor_scalar(qkv_al[:, :, :], qkv_raw[:, :, :], alpha1, None, ALU.mult)
            dve.tensor_scalar(fc1_al[:, :, :], fc1_raw[:, :, :], alpha2, None, ALU.mult).then_inc(setup, 1)
            dve.wait_ge(w_made, 1)
            dve.tensor_copy(w_qkv[:, :, :], ps_s[0][:, 0:3, :])
            dve.tensor_copy(w_fc1[:, :, :], ps_s[1][:, 0:RG, :])
            dve.tensor_tensor(b_fc1[:, :], ps_m[0][:, 3:4], b_fc1_in, ALU.add)
            dve.tensor_tensor(b_qkv[:, :], ps_m[0][:, 0:3], b_qkv_in, ALU.add).then_inc(setup, 1)
            dve.wait_ge(setup, 3)
            dve.tensor_scalar(q_bias[:, :], q_scale, b_qkv[:, 0:1], None, ALU.mult)
            dve.tensor_scalar(k_bias[:, :], head_mask, b_qkv[:, 1:2], None, ALU.mult).then_inc(w_ready, 1)
            dve.wait_ge(w_ready, 1)

            def conv(i, par, steps):
                if not there(i):
                    return
                for st in steps:
                    dy, dx = TAPS[st] if st < len(TAPS) else (1, 1)
                    view = xin[:, par, dy:dy + WS, dx:dx + CW]
                    if st == 0:
                        wait(dve, conv_step, i * STEPS_OF_CONV)
                        dve.wait_ge(x_in[par], (i + (2 - par)) * (8 * WR))
                        dve.tensor_scalar(acc[:, :, :], view, pos_w[:, 4:5], pos_b, ALU.mult, ALU.add).then_inc(conv_step, 1)
                        continue
                    dve.wait_ge(conv_step, i * STEPS_OF_CONV + st)
                    if st < len(TAPS):
                        dve.scalar_tensor_tensor(out=acc[:, :, :], in0=view, scalar=pos_w[:, 3 * dy + dx:3 * dy + dx + 1],
                                                 in1=acc[:, :, :], op0=ALU.mult, op1=ALU.add).then_inc(conv_step, 1)
                    else:
                        wait(dve, x2_done, i - 1)
                        turned = [a.rearrange("p y (w x) -> p w y x", x=WS) for a in (acc[:, :, :], view)]
                        dve.tensor_tensor(xs[:, par, :].rearrange("p (w y x) -> p w y x", y=WS, x=WS), *turned,
                                          ALU.add).then_inc(conv_step, 1)

            def top(i, rg):
                if not there(i):
                    return
                dve.wait_ge(s_made, i * 4 + (rg + 1))
                sc = ps_s[rg % 2][:, :, :].rearrange("p w (h m) -> p (w h) m", h=HEADS)
                dve.tensor_reduce(mx[:, rg, :], sc, AX.X, ALU.max).then_inc(max_done, 1)
                wait(dve, t_made, i * 8 + (rg * 2 - 6))
                dve.wait_ge(max_done, i * 4 + (rg + 1))
                dve.tensor_tensor(pr[:, rg], sc, mx[:, rg, :].unsqueeze(2).to_broadcast([P, WC * HEADS, N]),
                                  ALU.subtract).then_inc(sub_done, 1)

            def total(i, rg):
                if not there(i):
                    return
                dve.wait_ge(exp_done, i * 4 + (rg + 1))
                dve.tensor_reduce(sm[:, rg, :], pr[:, rg], AX.X, ALU.add).then_inc(sum_done, 1)
                dve.wait_ge(sum_done, i * 4 + (rg + 1))
                dve.reciprocal(rs[:, rg, :], sm[:, rg, :]).then_inc(rec_done, 1)

            def residual(i, par):
                if not there(i):
                    return
                dve.wait_ge(proj_made, i + 1)
                wait(dve, y_done, i - 1)
                dve.scalar_tensor_tensor(out=x2[:, par, :], in0=ps_m[1][:, :], scalar=b_proj, in1=xs[:, par, :],
                                         op0=ALU.add, op1=ALU.add).then_inc(x2_done, 1)

            def finish(i, par):
                if not there(i):
                    return
                dve.wait_ge(f2_made, i + 1)
                wait(dve, row_copied, i)
                dve.scalar_tensor_tensor(out=y_sb[:, :], in0=ps_m[0][:, :], scalar=b_fc2, in1=x2[:, par, :],
                                         op0=ALU.add, op1=ALU.add).then_inc(y_done, 1)

            def slot(i, par):
                o = 1 - par
                residual(i - 1, o)
                total(i, 1)
                conv(i + 1, o, range(9, 10))
                top(i, 2)

                conv(i + 2, par, range(0, 1))
                total(i, 2)
                top(i, 3)
                conv(i + 2, par, range(1, 3))

                total(i, 3)
                conv(i + 2, par, range(3, 5))
                top(i + 1, 0)
                conv(i + 2, par, range(5, 6))

                conv(i + 2, par, range(6, 7))
                total(i + 1, 0)
                top(i + 1, 1)
                conv(i + 2, par, range(7, 9))
                finish(i - 2, par)

            every_slot(dve, slot)


def attention_weights(a):
    import numpy as np
    C, WR, HID = 16, 8, 64
    f = np.float32

    def blocks(m):
        i, o = m.shape
        z = np.zeros((WR, i, WR, o), m.dtype)
        for r in range(WR):
            z[r, :, r, :] = m
        return z.reshape(WR * i, WR * o)

    def tile(v):
        return np.tile(np.asarray(v).reshape(-1), 128 // np.asarray(v).size).reshape(128, 1)

    qkv = a["qkv_w"]
    p = np.arange(128)
    row = (p // C) % 2
    head = (p // (C // 2)) % 2
    scale = (C // 2) ** -0.5
    vec = np.concatenate(
        [np.tile(a["pos_w"].reshape(C, 9), (WR, 1)), tile(a["pos_b"]), tile(a["alpha1"]), tile(a["beta1"]), tile(a["alpha2"]),
         tile(a["beta2"])] + [tile(a["qkv_b"][C * k:C * k + C]) for k in range(3)] +
        [tile(a["proj_b"]), tile(a["fc1_b"]), tile(a["fc2_b"])] +
        [np.where(row == r, scale, 0).astype(f).reshape(128, 1) for r in range(2)] +
        [np.where(head == h, 1, 0).astype(f).reshape(128, 1) for h in range(2)], axis=1).astype(f)
    fc2 = blocks(np.ascontiguousarray(a["fc2_w"].T)).reshape(WR * HID // 128, 128, 128).transpose(1, 0, 2)
    return dict(
        color=np.stack([blocks(a["color1"]), blocks(a["color2"])], axis=1),
        qkv=np.stack([blocks(np.ascontiguousarray(qkv[C * k:C * k + C].T)) for k in range(3)], axis=1),
        fc1=blocks(np.ascontiguousarray(a["fc1_w"].T)).reshape(128, 4, 128),
        proj=blocks(np.ascontiguousarray(a["proj_w"].T)),
        fc2=np.ascontiguousarray(fc2),
        ident=np.eye(128, dtype=f),
        vec=vec)


def surface_consts():
    import numpy as np
    P = 128
    profiles = {
        "ux": ([1, 2, 1], 8, (-1, 1)),
        "uy": ([-1, 0, 1], 8, (1, 2)),
        "uxx": ([1, 4, 6, 4, 1], 64, (1, -2)),
        "uxy": ([-1, -2, 0, 2, 1], 64, (-1, -2, 2, 1)),
        "uyy": ([1, 0, -2, 0, 1], 64, (1, 4, 6)),
    }
    mats = []
    for taps, div, weights in profiles.values():
        r = len(taps) // 2
        band = np.zeros((P, P), np.float32)
        for m in range(P):
            for o, v in enumerate(taps):
                k = m + o - r
                if 0 <= k < P:
                    band[k, m] = v / div
        mats += [w * band for w in weights]
    return np.stack(mats, axis=1).astype(np.float32)


def surface_mask(slots, edge_slot, halo, blocks, block_rows):
    import numpy as np
    m = np.zeros((128, slots), np.float32)
    m[halo:128 - halo, :] = 0.01
    m[:, edge_slot] = 0.0
    for b in range(blocks):
        m[b * block_rows + halo:(b + 1) * block_rows - halo, edge_slot] = 0.01
    return m


def surface_stage(nc, x1, u10, mats, mask, alpha_in, beta_in, STEPS):
    P = 128
    IMAGES, HP, W = x1.shape
    HALO = 2
    OWN = P - 2 * HALO
    KT = (HP - 2 * HALO) // OWN
    REST = HP - 2 * HALO - KT * OWN
    BLOCK = REST + 2 * HALO
    GI = 8
    HI = GI // 2
    GROUPS = IMAGES // GI
    UNITS = HI * KT + 1
    FIRST = HI // 2
    REST_UNIT = FIRST * KT
    TOTAL = GROUPS * STEPS * UNITS
    NM = mats.shape[1]
    EPS = 1e-6
    TAPS = {
        "p": [(-1, 0), (1, 1)],
        "q": [(-1, 2), (0, 3), (1, 2)],
        "A": [(-2, 4), (0, 5), (2, 4)],
        "B": [(-2, 6), (-1, 7), (1, 8), (2, 9)],
        "C": [(-2, 10), (-1, 11), (0, 12), (1, 11), (2, 10)],
    }

    def unit0(j):
        return j * KT + (1 if j >= FIRST else 0)

    with ExitStack() as ctx:
        def sb(name, shape, dt=F32):
            return ctx.enter_context(nc.sbuf_tensor(name, shape, dt))

        def sem(name):
            return ctx.enter_context(nc.semaphore(name))

        u = sb("surf_u", [P, UNITS, 2, W])
        parts = sb("surf_parts", [P, 2, 2, 2, W + 4], F32R)
        matf = sb("surf_matf", [P, NM, P])
        matr = sb("surf_matr", [P, NM, P], F32R)
        dt_mask = sb("surf_dt", [P, UNITS])
        ab = sb("surf_ab", [P, 2])
        absab = sb("surf_absab", [P, 2])
        clip_h = sb("surf_clip_h", [P, 2])
        bufs = {n: sb("surf_" + n, [P, 2, 2, W]) for n in
                ("pc", "qc", "Ac", "Bc", "Cc", "p2", "q2", "B2", "g", "rK", "rH", "nK", "m")}
        banks = [ctx.enter_context(nc.psum_tensor(f"surf_ps{i}", [P, 2, W], F32)) for i in range(4)]
        alpha, beta = absab[:, 0:1], absab[:, 1:2]

        init_loaded, init_set, init_done, mats_round = (sem(n) for n in ("init_loaded", "init_set", "init_done", "mats_round"))
        batches, moved, unit_ready, updated = sem("batches"), sem("moved"), sem("unit_ready"), sem("updated")
        hi_done, lo_done = sem("hi_done"), sem("lo_done")
        made = {n: sem("made_" + n) for n in "pqABC"}
        copied = {n: sem("copied_" + n) for n in "qABC"}
        clipped = {n: sem("clipped_" + n) for n in "pqABC"}
        squared = {n: sem("squared_" + n) for n in "pqB"}
        g_sum, ac_done, numk, pq_done, t12_done, numh = (sem(n) for n in ("g_sum", "ac_done", "numk", "pq_done", "t12_done", "numh"))
        den_squared, den_ln, g_ln, g_pow, pow_ln, rk_done, rh_done = (
            sem(n) for n in ("den_squared", "den_ln", "g_ln", "g_pow", "pow_ln", "rk_done", "rh_done"))
        t1_done, t2_done, m_done = sem("t1_done"), sem("t2_done"), sem("m_done")
        k_made, k_clipped, h_scaled, h_clipped, s_done, s_clipped, u_stepped = (
            sem(n) for n in ("k_made", "k_clipped", "h_scaled", "h_clipped", "s_done", "s_clipped", "u_stepped"))

        def flat(ap):
            return ap.rearrange("p t w -> p (t w)")

        def buf(n, par):
            return flat(bufs[n][:, par])

        def bank(name, par):
            return banks[(5 * par + list(TAPS).index(name)) % 4]

        def last_in_bank(j, par):
            names = list(TAPS)
            if j == 4:
                return names[0], 0
            o = 1 - par
            return names[max(x for x in range(5) if (5 * o + x) % 4 == (5 * par + j) % 4)], 1

        block = ctx.enter_context(nc.Block())

        @block.sync
        def _(sp):
            sp.dma_start(matf[:, :, :], mats).then_inc(init_loaded, 16)
            sp.dma_start(dt_mask[:, :], mask).then_inc(init_loaded, 16)
            sp.dma_start(ab[:, 0:1], alpha_in.to_broadcast([P, 1])).then_inc(init_loaded, 16)
            sp.dma_start(ab[:, 1:2], beta_in.to_broadcast([P, 1])).then_inc(init_loaded, 16)
            sp.wait_ge(init_done, 1)

            def landed(c):
                sp.wait_ge(moved, c)
                sp.sem_inc(batches, 1)

            def load_pair(g, j):
                for t in range(2):
                    img = g * GI + (j + t * HI)
                    for k in range(KT):
                        sp.dma_start(u[:, unit0(j) + k, t, :],
                                     x1[bass.ds(img, 1), OWN * k:OWN * k + P, :].rearrange("a p w -> p (a w)")).then_inc(moved, 16)

            def load_rests(g):
                for t in range(2):
                    for j in range(HI):
                        img = g * GI + (j + t * HI)
                        sp.dma_start(u[j * BLOCK:(j + 1) * BLOCK, REST_UNIT, t, :],
                                     x1[bass.ds(img, 1), OWN * KT:OWN * KT + BLOCK, :].rearrange("a p w -> p (a w)")).then_inc(moved, 16)

            def store_pair(g, j):
                for t in range(2):
                    img = g * GI + (j + t * HI)
                    for k in range(KT):
                        sp.dma_start(u10[bass.ds(img, 1), HALO + OWN * k:HALO + OWN * (k + 1), :].rearrange("a p w -> p (a w)"),
                                     u[HALO:P - HALO, unit0(j) + k, t, :]).then_inc(moved, 16)

            def store_rests(g):
                for t in range(2):
                    for j in range(HI):
                        img = g * GI + (j + t * HI)
                        sp.dma_start(u10[bass.ds(img, 1), HALO + OWN * KT:HALO + OWN * KT + REST, :].rearrange("a p w -> p (a w)"),
                                     u[j * BLOCK + HALO:(j + 1) * BLOCK - HALO, REST_UNIT, t, :]).then_inc(moved, 16)

            def exchange_pair(j):
                a, b = unit0(j), unit0(j) + KT - 1
                n = 0
                if KT > 1:
                    sp.dma_start(u[0:HALO, a + 1:b + 1], u[P - 2 * HALO:P - HALO, a:b]).then_inc(moved, 16)
                    sp.dma_start(u[P - HALO:P, a:b], u[HALO:2 * HALO, a + 1:b + 1]).then_inc(moved, 16)
                    n += 2
                sp.dma_start(u[HALO:HALO + 1, a], u[HALO + 1:HALO + 2, a]).then_inc(moved, 16)
                return n + 1

            def exchange_rest(j):
                b, r = unit0(j) + KT - 1, j * BLOCK
                sp.dma_start(u[r:r + HALO, REST_UNIT], u[P - 2 * HALO:P - HALO, b]).then_inc(moved, 16)
                sp.dma_start(u[P - HALO:P, b], u[r + HALO:r + 2 * HALO, REST_UNIT]).then_inc(moved, 16)
                return 2

            def last_rows():
                for j in range(HI):
                    r = j * BLOCK + HALO + REST - 1
                    sp.dma_start(u[r:r + 1, REST_UNIT], u[r - 1:r, REST_UNIT]).then_inc(moved, 16)
                return HI

            loads_pair, rests = 2 * KT, 2 * HI
            load_pair(0, 0)
            landed(16 * loads_pair)
            sp.sem_inc(unit_ready, KT)
            for j in range(1, FIRST):
                load_pair(0, j)
            load_rests(0)
            for j in range(FIRST, HI):
                load_pair(0, j)
            n0 = 16 * (loads_pair * HI + rests)
            sp.wait_ge(moved, n0)
            sp.sem_inc(unit_ready, UNITS - KT)

            per_pair = 3 if KT > 1 else 1
            EX = 16 * (per_pair * HI + 2 * HI + HI)
            STEP_A = REST_UNIT + 1

            def exchange(done, before):
                c = before
                for j in range(FIRST):
                    sp.wait_ge(updated, done + unit0(j) + KT)
                    c = c + 16 * exchange_pair(j)
                    landed(c)
                sp.wait_ge(updated, done + REST_UNIT + 1)
                c = c + 16 * last_rows()
                for j in range(FIRST):
                    c = c + 16 * exchange_rest(j)
                landed(c)
                sp.sem_inc(unit_ready, STEP_A - 1)
                for j in range(FIRST, HI):
                    sp.wait_ge(updated, done + unit0(j) + KT)
                    c = c + 16 * exchange_pair(j)
                    c = c + 16 * exchange_rest(j)
                    landed(c)
                sp.sem_inc(unit_ready, UNITS - STEP_A + 1)

            def boundary(g, done, before, load):
                c = before
                for j in range(FIRST):
                    sp.wait_ge(updated, done + unit0(j) + KT)
                    sp.dma_start(u[HALO:HALO + 1, unit0(j)], u[HALO + 1:HALO + 2, unit0(j)]).then_inc(moved, 16)
                    c = c + 16
                    landed(c)
                    store_pair(g, j)
                    c = c + 16 * loads_pair
                    landed(c)
                    if load:
                        load_pair(g + 1, j)
                        c = c + 16 * loads_pair
                        landed(c)
                sp.wait_ge(updated, done + REST_UNIT + 1)
                c = c + 16 * last_rows()
                landed(c)
                store_rests(g)
                c = c + 16 * rests
                landed(c)
                if load:
                    load_rests(g + 1)
                    c = c + 16 * rests
                    landed(c)
                    sp.sem_inc(unit_ready, STEP_A)
                for j in range(FIRST, HI):
                    sp.wait_ge(updated, done + unit0(j) + KT)
                    sp.dma_start(u[HALO:HALO + 1, unit0(j)], u[HALO + 1:HALO + 2, unit0(j)]).then_inc(moved, 16)
                    c = c + 16
                    landed(c)
                    store_pair(g, j)
                    c = c + 16 * loads_pair
                    landed(c)
                    if load:
                        load_pair(g + 1, j)
                        c = c + 16 * loads_pair
                        landed(c)
                if load:
                    sp.sem_inc(unit_ready, UNITS - STEP_A)

            BD = 16 * (2 * (loads_pair * HI + rests) + 2 * HI)
            GROUP_MOVES = (STEPS - 1) * EX + BD
            if GROUPS > 1:
                with sp.Fori(0, GROUPS - 1) as g:
                    with sp.Fori(0, STEPS - 1) as s:
                        exchange(g * (STEPS * UNITS) + s * UNITS, g * GROUP_MOVES + s * EX + n0)
                    boundary(g, g * (STEPS * UNITS) + (STEPS - 1) * UNITS, g * GROUP_MOVES + ((STEPS - 1) * EX + n0), True)
            last = GROUPS - 1
            with sp.Fori(0, STEPS - 1) as s:
                exchange(s * UNITS + last * STEPS * UNITS, s * EX + (last * GROUP_MOVES + n0))
            boundary(last, last * STEPS * UNITS + (STEPS - 1) * UNITS, last * GROUP_MOVES + (STEPS - 1) * EX + n0, False)

        @block.tensor
        def _(pe):
            pe.wait_ge(mats_round, 1)

            def unit(n, par, first):
                pe.wait_ge(lo_done, n + 1)
                for j, (name, taps) in enumerate(TAPS.items()):
                    ps = bank(name, par)
                    if not first or j == 4:
                        before, back = last_in_bank(j, par)
                        pe.wait_ge((clipped if before == "p" else copied)[before], n - back + 1)
                    count = 2 * len(taps)
                    for t in range(2):
                        i = 0
                        for off, mat in taps:
                            for part in range(2):
                                mm = pe.matmul(ps[:, t, :], matr[:, mat, :], parts[:, par, part, t, off + 2:off + 2 + W],
                                               start=(i == 0), stop=(i == count - 1))
                                i += 1
                    mm.then_inc(made[name], 1)

            unit(0, 0, True)
            unit(1, 1, False)
            with pe.Fori(2, TOTAL, 2) as n:
                unit(n, 0, False)
                unit(n + 1, 1, False)

        @block.scalar
        def _(act):
            act.preload_act_table_set("natural_log_exp_and_others")

            def slot(n, par, new=True, mid=True, nxt=True, wait_ready=True):
                o = 1 - par
                if mid:
                    act.wait_ge(made["C"], n)
                    if not isinstance(n, int) or n > 2:
                        act.wait_ge(s_done, n - 2)
                    act.activation(buf("Cc", o), flat(bank("C", o)[:, :, :]), ACT.Copy).then_inc(copied["C"], 1)
                    act.wait_ge(clipped["B"], n)
                    act.activation(buf("B2", o), buf("Bc", o), ACT.Square).then_inc(squared["B"], 1)
                if nxt:
                    act.activation(parts[:, o, 0, :, 2:W + 2], u[:, bass.ds((n + 1) % UNITS, 1), :, :].rearrange("p a t w -> p (a t) w"),
                                   ACT.Copy).then_inc(hi_done, 1)
                if mid:
                    act.wait_ge(g_sum, n)
                    act.activation(buf("rK", o), buf("g", o), ACT.Square, bias=1.0).then_inc(den_squared, 1)
                    act.activation(buf("rH", o), buf("g", o), ACT.Ln, bias=1.0 + EPS).then_inc(g_ln, 1)
                if new:
                    act.wait_ge(made["q"], n + 1)
                    act.activation(buf("qc", par), flat(bank("q", par)[:, :, :]), ACT.Copy).then_inc(copied["q"], 1)
                if mid:
                    act.wait_ge(den_squared, n)
                    act.activation(buf("rK", o), buf("rK", o), ACT.Ln, bias=EPS).then_inc(den_ln, 1)
                    act.wait_ge(g_ln, n)
                    act.activation(buf("rH", o), buf("rH", o), ACT.Exp, scale=1.5).then_inc(g_pow, 1)
                if new:
                    act.wait_ge(clipped["p"], n + 1)
                    act.activation(buf("p2", par), buf("pc", par), ACT.Square).then_inc(squared["p"], 1)
                    act.wait_ge(made["A"], n + 1)
                    act.activation(buf("Ac", par), flat(bank("A", par)[:, :, :]), ACT.Copy).then_inc(copied["A"], 1)
                if mid:
                    act.wait_ge(den_ln, n)
                    act.activation(buf("rK", o), buf("rK", o), ACT.Exp, scale=-1.0).then_inc(rk_done, 1)
                    act.wait_ge(g_pow, n)
                    act.activation(buf("rH", o), buf("rH", o), ACT.Ln, bias=EPS, scale=2.0).then_inc(pow_ln, 1)
                if new:
                    if wait_ready:
                        act.wait_ge(unit_ready, n + 3)
                    act.wait_ge(made["B"], n + 1)
                    act.activation(buf("Bc", par), flat(bank("B", par)[:, :, :]), ACT.Copy).then_inc(copied["B"], 1)
                    act.wait_ge(clipped["q"], n + 1)
                    act.activation(buf("q2", par), buf("qc", par), ACT.Square).then_inc(squared["q"], 1)
                if mid:
                    act.wait_ge(pow_ln, n)
                    act.activation(buf("rH", o), buf("rH", o), ACT.Exp, scale=-1.0).then_inc(rh_done, 1)

            act.wait_ge(unit_ready, 2)
            act.activation(parts[:, 0, 0, :, 2:W + 2], u[:, 0, :, :], ACT.Copy).then_inc(hi_done, 1)
            slot(0, 0, mid=False)
            slot(1, 1)
            slot(2, 0)
            slot(3, 1)
            with act.Fori(4, TOTAL - 2, 2) as n:
                slot(n, 0)
                slot(n + 1, 1)
            slot(TOTAL - 2, 0, wait_ready=False)
            slot(TOTAL - 1, 1, nxt=False, wait_ready=False)
            slot(TOTAL, 0, new=False, nxt=False)

        @block.gpsimd
        def _(pool):
            def slot(n, par):
                o = 1 - par
                g, p2, q2 = buf("g", o), buf("p2", o), buf("q2", o)
                nk, ac, cc, m = buf("nK", o), buf("Ac", o), buf("Cc", o), buf("m", o)
                pool.wait_ge(squared["q"], n)
                pool.tensor_tensor(g, p2, q2, ALU.add).then_inc(g_sum, 1)
                pool.wait_ge(clipped["q"], n)
                pool.tensor_tensor(m, buf("pc", o), buf("qc", o), ALU.mult).then_inc(pq_done, 1)
                pool.wait_ge(clipped["C"], n)
                pool.tensor_tensor(nk, ac, cc, ALU.mult).then_inc(ac_done, 1)
                pool.wait_ge(ac_done, n)
                pool.wait_ge(squared["B"], n)
                pool.tensor_tensor(nk, nk, buf("B2", o), ALU.subtract).then_inc(numk, 1)
                pool.wait_ge(t1_done, n)
                pool.wait_ge(t2_done, n)
                pool.tensor_tensor(p2, q2, p2, ALU.add).then_inc(t12_done, 1)
                pool.wait_ge(m_done, n)
                pool.wait_ge(t12_done, n)
                pool.tensor_tensor(cc, p2, m, ALU.add).then_inc(numh, 1)

            slot(1, 1)
            slot(2, 0)
            with pool.Fori(2, TOTAL, 2) as n:
                slot(n + 1, 1)
                slot(n + 2, 0)

        @block.vector
        def _(dve):
            dve.memset(parts[:, :, :, :, :].rearrange("p a b t w -> p (a b t w)").bitcast(F32), 0.0).then_inc(init_set, 1)
            dve.memset(u[:, REST_UNIT].rearrange("p t w -> p (t w)"), 0.0).then_inc(init_set, 1)
            dve.wait_ge(init_set, 2)
            dve.sem_inc(init_done, 1)
            dve.wait_ge(init_loaded, 64)
            dve.tensor_copy(matr[:, :, :], matf[:, :, :]).then_inc(mats_round, 1)
            dve.scalar_tensor_tensor(out=absab[:, :], in0=ab[:, :], scalar=-1.0, in1=ab[:, :], op0=ALU.mult, op1=ALU.max).then_inc(init_set, 1)
            dve.wait_ge(init_set, 3)

            CLIP = (10.0, -10.0, ALU.min, ALU.max)

            def low(n, o):
                dve.wait_ge(hi_done, n + 1)
                dve.tensor_tensor(parts[:, o, 1, :, 2:W + 2], u[:, bass.ds(n % UNITS, 1), :, :].rearrange("p a t w -> p (a t) w"),
                                  parts[:, o, 0, :, 2:W + 2].bitcast(F32), ALU.subtract).then_inc(lo_done, 1)

            def slot(n, par, new=True, mid=True, end=True, nxt=True):
                o = 1 - par
                if end:
                    dve.wait_ge(rk_done, n - 1)
                    dve.wait_ge(numk, n - 1)
                    dve.tensor_tensor(buf("nK", par), buf("nK", par), buf("rK", par), ALU.mult).then_inc(k_made, 1)
                if new:
                    dve.wait_ge(made["p"], n + 1)
                    dve.tensor_scalar(buf("pc", par), flat(bank("p", par)[:, :, :]), *CLIP).then_inc(clipped["p"], 1)
                if nxt:
                    low(n + 1, o)
                if mid:
                    dve.wait_ge(g_sum, n)
                    dve.wait_ge(clipped["C"], n)
                    dve.scalar_tensor_tensor(out=buf("p2", o), in0=buf("p2", o), scalar=1.0, in1=buf("Cc", o),
                                             op0=ALU.add, op1=ALU.mult).then_inc(t2_done, 1)
                if end:
                    dve.wait_ge(rh_done, n - 1)
                    dve.wait_ge(numh, n - 1)
                    dve.scalar_tensor_tensor(out=buf("Cc", par), in0=buf("Cc", par), scalar=beta, in1=buf("rH", par),
                                             op0=ALU.mult, op1=ALU.mult).then_inc(h_scaled, 1)
                    dve.wait_ge(k_made, n - 1)
                    dve.tensor_scalar(buf("nK", par), buf("nK", par), 5.0, -5.0, ALU.min, ALU.max).then_inc(k_clipped, 1)
                if mid:
                    dve.scalar_tensor_tensor(out=buf("q2", o), in0=buf("q2", o), scalar=1.0, in1=buf("Ac", o),
                                             op0=ALU.add, op1=ALU.mult).then_inc(t1_done, 1)
                if end:
                    dve.wait_ge(h_scaled, n - 1)
                    dve.tensor_scalar(buf("Cc", par), buf("Cc", par), clip_h[:, 0:1], clip_h[:, 1:2], ALU.min, ALU.max).then_inc(h_clipped, 1)
                if new:
                    dve.wait_ge(copied["q"], n + 1)
                    dve.tensor_scalar(buf("qc", par), buf("qc", par), *CLIP).then_inc(clipped["q"], 1)
                if mid:
                    dve.wait_ge(pq_done, n)
                    dve.scalar_tensor_tensor(out=buf("m", o), in0=buf("m", o), scalar=-2.0, in1=buf("Bc", o),
                                             op0=ALU.mult, op1=ALU.mult).then_inc(m_done, 1)
                if end:
                    dve.wait_ge(h_clipped, n - 1)
                    dve.wait_ge(k_clipped, n - 1)
                    dve.scalar_tensor_tensor(out=buf("nK", par), in0=buf("nK", par), scalar=alpha, in1=buf("Cc", par),
                                             op0=ALU.mult, op1=ALU.add).then_inc(s_done, 1)
                if new:
                    dve.wait_ge(copied["A"], n + 1)
                    dve.tensor_scalar(buf("Ac", par), buf("Ac", par), *CLIP).then_inc(clipped["A"], 1)
                if end:
                    dve.wait_ge(s_done, n - 1)
                    dve.tensor_scalar(buf("nK", par), buf("nK", par), 1.0, -1.0, ALU.min, ALU.max).then_inc(s_clipped, 1)
                if new:
                    dve.wait_ge(copied["B"], n + 1)
                    dve.tensor_scalar(buf("Bc", par), buf("Bc", par), *CLIP).then_inc(clipped["B"], 1)
                if end:
                    dve.wait_ge(s_clipped, n - 1)
                    un = u[:, bass.ds((n - 2) % UNITS, 1), :, :].rearrange("p a t w -> p (a t w)")
                    dve.scalar_tensor_tensor(out=un, in0=buf("nK", par), scalar=dt_mask[:, bass.ds((n - 2) % UNITS, 1)], in1=un,
                                             op0=ALU.mult, op1=ALU.add).then_inc(u_stepped, 1)
                if new:
                    dve.wait_ge(copied["C"], n + 1)
                    dve.tensor_scalar(buf("Cc", par), buf("Cc", par), *CLIP).then_inc(clipped["C"], 1)
                if end:
                    uv = u[:, bass.ds((n - 2) % UNITS, 1), :, :].rearrange("p a t w -> p (a t) w")
                    dve.wait_ge(u_stepped, n - 1)
                    dve.tensor_scalar(uv[:, :, 0:W:W - 1], uv[:, :, 1:W - 1:W - 3], 1.0, None, ALU.mult).then_inc(updated, 1)

            for i, v in enumerate((5.0, -5.0)):
                dve.tensor_scalar(clip_h[:, i:i + 1], beta, v, None, ALU.mult).then_inc(init_set, 1)
            dve.wait_ge(init_set, 5)
            low(0, 0)
            slot(0, 0, mid=False, end=False)
            slot(1, 1, end=False)
            with dve.Fori(2, TOTAL - 2, 2) as n:
                slot(n, 0)
                slot(n + 1, 1)
            slot(TOTAL - 2, 0)
            slot(TOTAL - 1, 1, nxt=False)
            slot(TOTAL, 0, new=False, nxt=False)
            slot(TOTAL + 1, 1, new=False, mid=False, nxt=False)


RIN, ROUT = 8, 6


def conv_stage(nc, name, src, dst, weights, bias, relu, residual=None, mix_with=None, mixed=None, dst_pad=0):
    P = 128
    B, C, HP, W = src.shape
    PAD = 2
    H = HP - 2 * PAD
    M = C * ROUT
    NB = 4
    TILES = -(-H // ROUT)
    LOOPS = (TILES - 1) // NB
    with ExitStack() as ctx:
        def sb(n, shape):
            return ctx.enter_context(nc.sbuf_tensor(f"{name}_{n}", shape, F32))

        def sem(n):
            return ctx.enter_context(nc.semaphore(f"{name}_{n}"))

        w_sb = sb("w", [P, 3, M])
        b_sb = sb("b", [M, 1])
        rows = sb("rows", [P, NB, B, W + 2])
        outs = sb("outs", [M, NB, B, W])
        res = sb("res", [M, NB, B, W]) if residual is not None else None
        us = sb("us", [P, NB, B, W]) if mix_with is not None else None
        xs = sb("xs", [P, NB, B, W]) if mix_with is not None else None
        ps = [ctx.enter_context(nc.psum_tensor(f"{name}_ps{i}", [M, B, W], F32)) for i in range(2)]
        w_loaded, padded = sem("w_loaded"), sem("padded")
        loaded = [sem(f"loaded{b}") for b in range(NB)]
        stored = [sem(f"stored{b}") for b in range(NB)]
        scaled, mix_done, conv_done, out_done = sem("scaled"), sem("mix_done"), sem("conv_done"), sem("out_done")
        if mixed is not None:
            y_stored = [sem(f"y_stored{b}") for b in range(NB)]

        def wait(eng, s, value):
            if not isinstance(value, int) or value > 0:
                eng.wait_ge(s, value)

        def every_tile(eng, body):
            for b in range(NB):
                body(0, b, ROUT * b)
            if LOOPS > 1:
                with eng.Fori(1, LOOPS) as i:
                    for b in range(NB):
                        body(i, b, i * (NB * ROUT) + ROUT * b)
            for t in range(NB * LOOPS, TILES):
                body(t // NB, t % NB, min(ROUT * t, H - ROUT))

        def dram_rows(a, b, row, n):
            return a[b, :, bass.ds(row, n), :]

        block = ctx.enter_context(nc.Block())

        @block.sync
        def _(sp):
            sp.dma_start(w_sb[:, :, :], weights).then_inc(w_loaded, 16)
            sp.dma_start(b_sb[:, :], bias).then_inc(w_loaded, 16)
            sp.wait_ge(padded, 1)

            def body(i, b, row):
                t = i * NB + b
                if mix_with is None:
                    wait(sp, conv_done, t - NB + 1)
                    for bb in range(B):
                        sp.dma_start(rows[:, b, bb, 1:W + 1], dram_rows(src, bb, row + PAD - 1, RIN)).then_inc(loaded[b], 16)
                else:
                    wait(sp, mix_done, t - NB + 1)
                    for bb in range(B):
                        sp.dma_start(us[:, b, bb, :], dram_rows(src, bb, row + PAD - 1, RIN)).then_inc(loaded[b], 16)
                        sp.dma_start(xs[:, b, bb, :], dram_rows(mix_with, bb, row + PAD - 1, RIN)).then_inc(loaded[b], 16)
                if residual is not None:
                    wait(sp, out_done, t - NB + 1)
                    for bb in range(B):
                        sp.dma_start(res[:, b, bb, :], dram_rows(residual, bb, row + PAD, ROUT)).then_inc(loaded[b], 16)

            every_tile(sp, body)

        NLOAD = 16 * B * (1 + (mix_with is not None) + (residual is not None))

        @block.tensor
        def _(pe):
            pe.wait_ge(w_loaded, 32)

            def body(i, b, row):
                t = i * NB + b
                if mix_with is None:
                    pe.wait_ge(loaded[b], (i + 1) * NLOAD)
                else:
                    pe.wait_ge(mix_done, t + 1)
                wait(pe, out_done, t - 1)
                for bb in range(B):
                    for dx in range(3):
                        mm = pe.matmul(ps[b % 2][:, bb, :], w_sb[:, dx, :], rows[:, b, bb, dx:dx + W],
                                       start=(dx == 0), stop=(dx == 2))
                mm.then_inc(conv_done, 1)

            every_tile(pe, body)

        @block.vector
        def _(dve):
            dve.memset(rows[:, :, :, 0:W + 2:W + 1].rearrange("p n b w -> p (n b) w"), 0.0).then_inc(padded, 1)
            if mix_with is not None:
                dve.wait_ge(padded, 1)
            if residual is not None:
                dve.wait_ge(w_loaded, 32)

            def mix_body(i, b, row):
                t = i * NB + b
                dve.wait_ge(loaded[b], (i + 1) * NLOAD)
                dve.tensor_scalar(xs[:, b], xs[:, b], 0.3, None, ALU.mult).then_inc(scaled, 1)
                wait(dve, y_stored[b], i * (16 * B))
                wait(dve, conv_done, t - NB + 1)
                dve.wait_ge(scaled, t + 1)
                dve.scalar_tensor_tensor(out=rows[:, b, :, 1:W + 1], in0=us[:, b], scalar=0.7, in1=xs[:, b],
                                         op0=ALU.mult, op1=ALU.add).then_inc(mix_done, 1)

            def sum_body(i, b, row):
                t = i * NB + b
                dve.wait_ge(conv_done, t + 1)
                dve.wait_ge(loaded[b], (i + 1) * NLOAD)
                wait(dve, stored[b], i * (16 * B))
                dve.scalar_tensor_tensor(out=outs[:, b], in0=ps[b % 2][:, :, :], scalar=b_sb[:, 0:1], in1=res[:, b],
                                         op0=ALU.add, op1=ALU.add).then_inc(out_done, 1)

            if mix_with is not None:
                every_tile(dve, mix_body)
            if residual is not None:
                every_tile(dve, sum_body)

        @block.scalar
        def _(act):
            act.wait_ge(w_loaded, 32)

            def body(i, b, row):
                t = i * NB + b
                if relu:
                    act.wait_ge(conv_done, t + 1)
                    wait(act, stored[b], i * (16 * B))
                    act.activation(outs[:, b].rearrange("p b w -> p (b w)"), ps[b % 2][:, :, :].rearrange("p b w -> p (b w)"),
                                   ACT.Relu, bias=b_sb[:, 0:1]).then_inc(out_done, 1)
                act.wait_ge(out_done, t + 1)
                if isinstance(i, int) and t == TILES - 1:
                    act.wait_ge(stored[(t - 1) % NB], ((t - 1) // NB + 1) * (16 * B))
                for bb in range(B):
                    act.dma_start(dram_rows(dst, bb, row + dst_pad, ROUT), outs[:, b, bb, :]).then_inc(stored[b], 16)

            every_tile(act, body)
            for b in range(NB):
                act.wait_ge(stored[b], ((TILES - 1 - b) // NB + 1) * (16 * B))

        if mixed is not None:
            @block.gpsimd
            def _(pool):
                def body(i, b, row):
                    t = i * NB + b
                    pool.wait_ge(mix_done, t + 1)
                    if not isinstance(i, int) or t > 0:
                        pool.wait_ge(y_stored[(b - 1) % NB], (i + 1 if b else i) * (16 * B))
                    for bb in range(B):
                        pool.dma_start(dram_rows(mixed, bb, row + PAD - 1, RIN), rows[:, b, bb, 1:W + 1]).then_inc(y_stored[b], 16)

                every_tile(pool, body)
                for b in range(NB):
                    pool.wait_ge(y_stored[b], ((TILES - 1 - b) // NB + 1) * (16 * B))


def conv_weights(w):
    import numpy as np
    co, ci = w.shape[:2]
    m = np.zeros((ci, RIN, 3, co, ROUT), w.dtype)
    for r in range(ROUT):
        for dy in range(3):
            m[:, r + dy, :, :, r] = w[:, :, dy, :].transpose(1, 2, 0)
    return m.reshape(ci * RIN, 3, co * ROUT)


def conv_bias(b):
    import numpy as np
    return np.repeat(b, ROUT).reshape(-1, 1)


def clear_halos(nc, zeros, arrays):
    with nc.semaphore("halos_cleared") as cleared, nc.semaphore("zeroed") as zeroed, \
            nc.sbuf_tensor("zero_rows", [64, zeros], F32) as rows, nc.Block() as block:
        @block.vector
        def _(dve):
            dve.memset(rows[:, :], 0.0).then_inc(zeroed, 1)

        @block.sync
        def _(sp):
            sp.wait_ge(zeroed, 1)
            for a in arrays:
                h = a.shape[2]
                images = a.rearrange("b c h w -> (b c) h w")
                for r in (0, h - 2):
                    sp.dma_start(images[:, r:r + 2, :].rearrange("i r w -> i (r w)"), rows[:, :]).then_inc(cleared, 16)
            sp.wait_ge(cleared, 16 * 2 * len(arrays))


def build(nc, ins, out):
    B, C, H, W = out.shape

    def scratch(name):
        return nc.dram_tensor(name, (B, C, H + 4, W), F32, kind="Internal").ap()

    attended, flowed, mixed, hidden, middle = (scratch(n) for n in ("attended", "flowed", "mixed", "hidden", "middle"))
    clear_halos(nc, 2 * W, (attended, flowed, hidden, middle))
    attention_stage(nc, ins["x"], attended, {n[4:]: ins[n] for n in ins if n.startswith("att_")})

    def images(a):
        return a.rearrange("b c h w -> (b c) h w")

    surface_stage(nc, images(attended), images(flowed), ins["surf_mats"], ins["surf_mask"], ins["alpha"], ins["beta"], STEPS)
    conv_stage(nc, "conv1", flowed, hidden, ins["w_conv1"], ins["b_conv1"], True, mix_with=attended, mixed=mixed, dst_pad=2)
    conv_stage(nc, "conv2", hidden, middle, ins["w_conv2"], ins["b_conv2"], False, residual=mixed, dst_pad=2)
    conv_stage(nc, "conv3", middle, hidden, ins["w_conv3"], ins["b_conv3"], True, dst_pad=2)
    conv_stage(nc, "conv4", hidden, out, ins["w_conv4"], ins["b_conv4"], False, residual=middle)


def kernel(**inputs):
    import numpy as _np
    import concourse.bacc as _bacc
    from concourse.bass_utils import run_bass_kernel_spmd as _run

    given = {n: _np.asarray(a) for n, a in inputs.items()}
    H = given["x"].shape[2]
    own, halo = 124, 2
    tiles = H // own
    rest = H - own * tiles
    arrays = {
        "x": _np.pad(given["x"], ((0, 0), (0, 0), (1, 1), (1, 1))),
        "surf_mats": surface_consts(),
        "surf_mask": surface_mask(4 * tiles + 1, 2 * tiles, halo, 4, rest + 2 * halo),
        "alpha": given["L1_conv_alpha_param"].reshape(1, 1),
        "beta": given["L1_conv_beta_param"].reshape(1, 1),
    }
    l0 = {n[len("L0_conv_"):]: a for n, a in given.items() if n.startswith("L0_conv_")}
    arrays.update({"att_" + n: a for n, a in attention_weights(l0).items()})
    for k, n in enumerate(("L2_conv_%s1", "L2_conv_%s2", "L3_conv_%s1", "L3_conv_%s2")):
        arrays[f"w_conv{k + 1}"] = conv_weights(given[n % "w"])
        arrays[f"b_conv{k + 1}"] = conv_bias(given[n % "b"])
    arrays = {n: _np.ascontiguousarray(a) for n, a in arrays.items()}

    nc = _bacc.Bacc("TRN2", target_bir_lowering=False, num_devices=1)
    ins = {n: nc.dram_tensor("in_" + n, a.shape, F32, kind="ExternalInput").ap() for n, a in arrays.items()}
    out = nc.dram_tensor("out_0", given["x"].shape, F32, kind="ExternalOutput").ap()
    build(nc, ins, out)
    r = _run(nc, [{"in_" + n: a for n, a in arrays.items()}], core_ids=[0])
    return r.results[0]["out_0"]
```
